# Optimizing a Trainium2 kernel written in Bass

```python
import numpy as np
import jax
import jax.numpy as jnp

def _softmax(x, axis=-1):
    return jax.nn.softmax(x, axis=axis)

def _gelu(x):
    return jax.nn.gelu(x, approximate=True)

def _silu(x):
    return jax.nn.silu(x)

def _sigmoid(x):
    return jax.nn.sigmoid(x)

def _layernorm(x, axis=-1, eps=1e-05):
    m = jnp.mean(x, axis=axis, keepdims=True)
    v = jnp.var(x, axis=axis, keepdims=True)
    return (x - m) / jnp.sqrt(v + eps)

def _scatter_add(tgt, idx, src, axis=0):
    return tgt.at[idx].add(src)

def _segment_sum(src, seg, n):
    return jax.ops.segment_sum(src, seg, n)
kernel_name = 'mk_adj_preln_d4_adj_r2_4eaa95'

def setup_inputs(seed: int=0):
    np.random.seed(seed)
    _w = jnp.asarray

    def _rec_inputs():
        import jax
        import jax.numpy as jnp
        _gk = jax.random.key(seed)
        x = -0.0005207 + 1.001 * jax.random.normal(jax.random.fold_in(_gk, 1), (64, 128, 128), jnp.float32)
        _w = (1.0 + jnp.arange(128, dtype=jnp.float32)) ** (-0.5)
        _w = _w / _w.mean()
        _pij = jnp.clip(0.0625 * _w[:, None] * _w[None, :], 0.0, 1.0)
        _a = jax.random.uniform(jax.random.fold_in(_gk, 2), (64, 128, 128)) < _pij
        _a = jnp.logical_or(_a, jnp.eye(128, dtype=bool))
        _af = _a.astype(jnp.float32)
        _af = _af * jax.random.uniform(jax.random.fold_in(_gk, 3), (64, 128, 128), jnp.float32, 0.05, 1)
        adj = _af
        _nm = jnp.ones((64, 128), dtype=bool)
        nodemask = jnp.where(_nm, 1.0, 0.0).astype(jnp.float32)
        return (x, adj, nodemask)
    x, adj, nodemask = _rec_inputs()

    def _L0_gnn_setup():
        import jax, jax.numpy as jnp
        import numpy as np
        B, N, D = (2, 2048, 128)
        key = jax.random.key(seed)
        ks = jax.random.split(key, 6)
        return {'hidden': jax.random.normal(ks[0], (B, N, D), dtype=jnp.float32), 'mask': jax.random.uniform(ks[1], (B, N, N), dtype=jnp.float32), 'W_w': jax.random.normal(ks[2], (D, D), dtype=jnp.float32) * 0.05, 'W_b': jax.random.normal(ks[3], (D,), dtype=jnp.float32) * 0.05, 'a_w': jax.random.normal(ks[4], (2 * D,), dtype=jnp.float32) * 0.05, 'a_b': jax.random.normal(ks[5], (1,), dtype=jnp.float32) * 0.05}
    _L0_gnn_all = _L0_gnn_setup()
    _L0_gnn_in = {k: v for k, v in _L0_gnn_all.items() if k in ('W_w', 'W_b', 'a_w', 'a_b')}
    del _L0_gnn_all

    def _L1_gnn_setup():
        import math
        import jax, jax.numpy as jnp
        import numpy as np
        B, N, D, H = (32, 256, 128, 8)
        HD = D // H
        key = jax.random.key(seed)
        ks = jax.random.split(key, 9)
        h = jax.random.normal(ks[0], (B, N, D), dtype=jnp.float32)
        edge = jax.random.normal(ks[1], (B, N, N), dtype=jnp.float32)
        adj = jax.random.uniform(ks[2], (B, N, N)) < 0.5
        adj_mask = adj | jnp.eye(N, dtype=bool)[None]
        s = 1.0 / math.sqrt(D)
        W_q = jax.random.normal(ks[3], (D, D), dtype=jnp.float32) * s
        W_k = jax.random.normal(ks[4], (D, D), dtype=jnp.float32) * s
        W_v = jax.random.normal(ks[5], (D, D), dtype=jnp.float32) * s
        W_e = jax.random.normal(ks[6], (H, 1), dtype=jnp.float32)
        W_o = jax.random.normal(ks[7], (D, D), dtype=jnp.float32) * s
        return {'h': h, 'edge': edge, 'adj_mask': adj_mask, 'W_q': W_q, 'W_k': W_k, 'W_v': W_v, 'W_e': W_e, 'W_o': W_o}
    _L1_gnn_all = _L1_gnn_setup()
    _L1_gnn_in = {k: v for k, v in _L1_gnn_all.items() if k in ('W_q', 'W_k', 'W_v', 'W_e', 'W_o')}
    del _L1_gnn_all

    def _L2_gnn_setup():
        import jax, jax.numpy as jnp
        import numpy as np
        GROUPS = [list(range(25)), [0, 1, 2, 3, 4, 5, 6, 7, 8], [0, 9, 10, 11, 12, 13, 14], [6, 7, 8, 12, 13, 14], [3, 4, 5, 9, 10, 11]]
        B, N, D_IN, D_HID = (4096, 25, 128, 256)

        def _graph_conv(x, adj, W, b):
            n = adj.shape[-1]
            A = adj + jnp.eye(n, dtype=adj.dtype)
            deg = jnp.sum(A, axis=-1)
            deg_safe = jnp.where(deg == 0, 1.0, deg)
            dinv = jnp.where(deg == 0, 0.0, deg_safe ** (-0.5))
            norm_adj = dinv[:, :, None] * A * dinv[:, None, :]
            support = jnp.einsum('bnd,de->bne', x, W)
            out = jnp.einsum('bnm,bme->bne', norm_adj, support) + b
            return jax.nn.relu(out)
        key = jax.random.key(seed)
        ks = jax.random.split(key, 7)
        s1 = float(np.sqrt(6.0 / (D_IN + D_HID)))
        s2 = float(np.sqrt(6.0 / (D_HID + D_IN)))
        return {'x': jax.random.normal(ks[0], (B, N, D_IN), dtype=jnp.float32), 'adj': jax.random.uniform(ks[1], (B, N, N), dtype=jnp.float32), 'W1': jax.random.uniform(ks[2], (5, D_IN, D_HID), jnp.float32, -s1, s1), 'b1': jnp.zeros((5, D_HID), dtype=jnp.float32), 'W2': jax.random.uniform(ks[3], (5, D_HID, D_IN), jnp.float32, -s2, s2), 'b2': jnp.zeros((5, D_IN), dtype=jnp.float32), 'fusion_w': jnp.ones((5,), dtype=jnp.float32)}
    _L2_gnn_all = _L2_gnn_setup()
    _L2_gnn_in = {k: v for k, v in _L2_gnn_all.items() if k in ('W1', 'b1', 'W2', 'b2', 'fusion_w')}
    del _L2_gnn_all

    def _L3_gnn_setup():
        import jax, jax.numpy as jnp
        import numpy as np
        B, N, D, C, L = (64, 256, 128, 128, 5)
        EDGE_P = 0.02

        def _gru_cell(m, h, w_ih, w_hh, b_ih, b_hh):
            gi = m @ w_ih.T + b_ih
            gh = h @ w_hh.T + b_hh
            i_r, i_z, i_n = jnp.split(gi, 3, axis=-1)
            h_r, h_z, h_n = jnp.split(gh, 3, axis=-1)
            r = jax.nn.sigmoid(i_r + h_r)
            z = jax.nn.sigmoid(i_z + h_z)
            n = jnp.tanh(i_n + r * h_n)
            return (1.0 - z) * n + z * h
        key = jax.random.key(seed)
        ks = jax.random.split(key, 8)
        x = jax.random.normal(ks[0], (B, N, D), dtype=jnp.float32)
        adj = (jax.random.uniform(ks[1], (B, N, N)) < EDGE_P).astype(jnp.float32)
        mask = jnp.ones((B, N), dtype=jnp.float32)
        s = 1.0 / np.sqrt(C).astype(np.float32)
        weight = jax.random.uniform(ks[2], (L, C, C), minval=-s, maxval=s, dtype=jnp.float32)
        w_ih = jax.random.uniform(ks[3], (3 * C, C), minval=-s, maxval=s, dtype=jnp.float32)
        w_hh = jax.random.uniform(ks[4], (3 * C, C), minval=-s, maxval=s, dtype=jnp.float32)
        b_ih = jax.random.uniform(ks[5], (3 * C,), minval=-s, maxval=s, dtype=jnp.float32)
        b_hh = jax.random.uniform(ks[6], (3 * C,), minval=-s, maxval=s, dtype=jnp.float32)
        return dict(x=x, adj=adj, mask=mask, weight=weight, w_ih=w_ih, w_hh=w_hh, b_ih=b_ih, b_hh=b_hh)
    _L3_gnn_all = _L3_gnn_setup()
    _L3_gnn_in = {k: v for k, v in _L3_gnn_all.items() if k in ('weight', 'w_ih', 'w_hh', 'b_ih', 'b_hh')}
    del _L3_gnn_all
    return {'x': x, 'adj': adj, 'nodemask': nodemask, 'L0_gnn_W_w': _L0_gnn_in['W_w'], 'L0_gnn_W_b': _L0_gnn_in['W_b'], 'L0_gnn_a_w': _L0_gnn_in['a_w'], 'L0_gnn_a_b': _L0_gnn_in['a_b'], 'L1_gnn_W_q': _L1_gnn_in['W_q'], 'L1_gnn_W_k': _L1_gnn_in['W_k'], 'L1_gnn_W_v': _L1_gnn_in['W_v'], 'L1_gnn_W_e': _L1_gnn_in['W_e'], 'L1_gnn_W_o': _L1_gnn_in['W_o'], 'L2_gnn_W1': _L2_gnn_in['W1'], 'L2_gnn_b1': _L2_gnn_in['b1'], 'L2_gnn_W2': _L2_gnn_in['W2'], 'L2_gnn_b2': _L2_gnn_in['b2'], 'L2_gnn_fusion_w': _L2_gnn_in['fusion_w'], 'L3_gnn_weight': _L3_gnn_in['weight'], 'L3_gnn_w_ih': _L3_gnn_in['w_ih'], 'L3_gnn_w_hh': _L3_gnn_in['w_hh'], 'L3_gnn_b_ih': _L3_gnn_in['b_ih'], 'L3_gnn_b_hh': _L3_gnn_in['b_hh']}

def reference(x, adj, nodemask, L0_gnn_W_w, L0_gnn_W_b, L0_gnn_a_w, L0_gnn_a_b, L1_gnn_W_q, L1_gnn_W_k, L1_gnn_W_v, L1_gnn_W_e, L1_gnn_W_o, L2_gnn_W1, L2_gnn_b1, L2_gnn_W2, L2_gnn_b2, L2_gnn_fusion_w, L3_gnn_weight, L3_gnn_w_ih, L3_gnn_w_hh, L3_gnn_b_ih, L3_gnn_b_hh):
    import jax
    import jax.numpy as jnp

    def _L0_gnn_ref(hidden, mask, W_w, W_b, a_w, a_b):
        import jax, jax.numpy as jnp
        import numpy as np
        B, N, D = (2, 2048, 128)
        h = jnp.einsum('bnd,ed->bne', hidden, W_w) + W_b
        Dh = h.shape[-1]
        a1, a2 = (a_w[:Dh], a_w[Dh:])
        e = h @ a1
        f = h @ a2
        logits = e[:, :, None] + f[:, None, :] + a_b[0]
        u = mask * jnp.exp(logits)
        a = u / jnp.sum(u, axis=2, keepdims=True)
        h_prime = jnp.einsum('bnm,bmd->bnd', a, h)
        return h_prime

    def _L1_gnn_ref(h, edge, adj_mask, W_q, W_k, W_v, W_e, W_o):
        import math
        import jax, jax.numpy as jnp
        import numpy as np
        B, N, D, H = (32, 256, 128, 8)
        HD = D // H
        b, n, _ = h.shape
        q = (h @ W_q.T).reshape(b, n, H, HD).transpose(0, 2, 1, 3)
        k = (h @ W_k.T).reshape(b, n, H, HD).transpose(0, 2, 1, 3)
        v = (h @ W_v.T).reshape(b, n, H, HD).transpose(0, 2, 1, 3)
        edge_bias = jnp.einsum('bij,h->bhij', edge, W_e[:, 0])
        scores = jnp.einsum('bhid,bhjd->bhij', q, k) / math.sqrt(HD) + edge_bias
        scores = jnp.where(adj_mask[:, None], scores, -jnp.inf)
        attn = jax.nn.softmax(scores, axis=-1)
        out = jnp.einsum('bhij,bhjd->bhid', attn, v)
        out = out.transpose(0, 2, 1, 3).reshape(b, n, D)
        return out @ W_o.T

    def _L2_gnn_ref(x, adj, W1, b1, W2, b2, fusion_w):
        import jax, jax.numpy as jnp
        import numpy as np
        GROUPS = [list(range(25)), [0, 1, 2, 3, 4, 5, 6, 7, 8], [0, 9, 10, 11, 12, 13, 14], [6, 7, 8, 12, 13, 14], [3, 4, 5, 9, 10, 11]]
        B, N, D_IN, D_HID = (4096, 25, 128, 256)

        def _graph_conv(x, adj, W, b):
            n = adj.shape[-1]
            A = adj + jnp.eye(n, dtype=adj.dtype)
            deg = jnp.sum(A, axis=-1)
            deg_safe = jnp.where(deg == 0, 1.0, deg)
            dinv = jnp.where(deg == 0, 0.0, deg_safe ** (-0.5))
            norm_adj = dinv[:, :, None] * A * dinv[:, None, :]
            support = jnp.einsum('bnd,de->bne', x, W)
            out = jnp.einsum('bnm,bme->bne', norm_adj, support) + b
            return jax.nn.relu(out)
        norm_w = jax.nn.softmax(fusion_w)
        fused = jnp.zeros_like(x)
        for g, idx_list in enumerate(GROUPS):
            idx = jnp.asarray(idx_list)
            x_g = x[:, idx, :]
            adj_g = adj[:, idx][:, :, idx]
            h = _graph_conv(x_g, adj_g, W1[g], b1[g])
            out_g = _graph_conv(h, adj_g, W2[g], b2[g])
            fused = fused.at[:, idx, :].add(norm_w[g] * out_g)
        return fused

    def _L3_gnn_ref(x, adj, mask, weight, w_ih, w_hh, b_ih, b_hh):
        import jax, jax.numpy as jnp
        import numpy as np
        B, N, D, C, L = (64, 256, 128, 128, 5)
        EDGE_P = 0.02

        def _gru_cell(m, h, w_ih, w_hh, b_ih, b_hh):
            gi = m @ w_ih.T + b_ih
            gh = h @ w_hh.T + b_hh
            i_r, i_z, i_n = jnp.split(gi, 3, axis=-1)
            h_r, h_z, h_n = jnp.split(gh, 3, axis=-1)
            r = jax.nn.sigmoid(i_r + h_r)
            z = jax.nn.sigmoid(i_z + h_z)
            n = jnp.tanh(i_n + r * h_n)
            return (1.0 - z) * n + z * h
        A = (adj != 0).astype(x.dtype)
        h = x
        for l in range(weight.shape[0]):
            m = jnp.einsum('bnd,de->bne', h, weight[l])
            agg = jnp.einsum('bij,bid->bjd', A, m)
            h = _gru_cell(agg, h, w_ih, w_hh, b_ih, b_hh)
        return h * mask[..., None]
    h = jnp.maximum(_layernorm(x, axis=-1), 0.0)
    x = x + _L0_gnn_ref(h, adj, L0_gnn_W_w, L0_gnn_W_b, L0_gnn_a_w, L0_gnn_a_b)
    h = jnp.maximum(_layernorm(x, axis=-1), 0.0)
    x = x + _L1_gnn_ref(h, adj, adj, L1_gnn_W_q, L1_gnn_W_k, L1_gnn_W_v, L1_gnn_W_e, L1_gnn_W_o)
    h = jnp.maximum(_layernorm(x, axis=-1), 0.0)
    x = x + _L2_gnn_ref(h, adj, L2_gnn_W1, L2_gnn_b1, L2_gnn_W2, L2_gnn_b2, L2_gnn_fusion_w)
    h = jnp.maximum(_layernorm(x, axis=-1), 0.0)
    x = x + _L3_gnn_ref(h, adj, nodemask, L3_gnn_weight, L3_gnn_w_ih, L3_gnn_w_hh, L3_gnn_b_ih, L3_gnn_b_hh)
    return x

_drawn_inputs = setup_inputs


def setup_inputs(seed=0):
    import zlib

    import numpy as np

    out = dict(_drawn_inputs(seed))
    spreads = {'L2_gnn_b1': (0.0, 0.8), 'L2_gnn_b2': (0.0, 0.8), 'L2_gnn_fusion_w': (1.0, 0.6)}
    factors = {}
    for name, (base, spread) in spreads.items():
        noise = np.random.default_rng([zlib.crc32(name.encode()), seed]).standard_normal(out[name].shape)
        drawn = base * np.exp(spread * noise) if base else spread * noise
        out[name] = jnp.asarray(drawn.astype(out[name].dtype))
    for name, factor in factors.items():
        out[name] = (out[name] * factor).astype(out[name].dtype)
    return out
```

```python
from contextlib import ExitStack

import numpy as np

import concourse.bass as bass
from concourse import mybir

F32 = mybir.dt.float32
F32R = mybir.dt.float32r
BF16 = mybir.dt.bfloat16
ALU = mybir.AluOpType
ACT = mybir.ActivationFunctionType
AXIS = mybir.AxisListType

B = 64
P = 128
EPS = 1e-5
GROUP = 4
NG = B // GROUP
W = GROUP * P
MASKED = -1e30

H = 8
HD = P // H
PAIR = 2
NP = B // PAIR
HC = 4
CH = PAIR * H // HC

GROUPS = [list(range(25)), [0, 1, 2, 3, 4, 5, 6, 7, 8], [0, 9, 10, 11, 12, 13, 14], [6, 7, 8, 12, 13, 14],
          [3, 4, 5, 9, 10, 11]]
NN = 25
HID = 256
SLOT = 32
ROWS = [(n, 1) for n in range(9)] + [(n, 2) for n in range(9, 15)] + [(0, 2)] + \
       [(n, 4) for n in (3, 4, 5)] + [(n, 3) for n in (6, 7, 8)] + [(n, 4) for n in (9, 10, 11)] + \
       [(n, 3) for n in (12, 13, 14)]
RUNS = [(0, 0, 15), (15, 0, 1), (16, 3, 12)]
SPANS = {1: [(0, 9)], 2: [(9, 16)], 3: [(19, 22), (25, 28)], 4: [(16, 19), (22, 25)]}
TILES = 4
BG = 4 * TILES
NB = B // BG

LAYERS = 5
GATES = 3

_SIZES = [("ww", P), ("wwT", P), ("bcol", 1), ("acol", 2), ("ab", 1), ("brow", P),
          ("wqT", P), ("wkT", P), ("wvT", P), ("woT", P), ("we", H),
          ("w1", 5 * HID), ("b1", 10), ("w2", 10 * P), ("b2", 5), ("fw", 5),
          ("gwT", LAYERS * P), ("wihT", GATES * P), ("whhT", GATES * P), ("bih", GATES), ("bhh", GATES), ("nmask", B)]
COL, _at = {}, 0
for _n, _s in _SIZES:
    COL[_n] = (_at, _at + _s)
    _at += _s
NCOL = _at
FIRST = COL["wqT"][0]


class Unit:

    def __init__(self, i, p, U=2):
        self.i, self.p, self.U = i, p, U

    @property
    def n(self):
        return self.U * self.i + self.p

    def back(self, k):
        q = self.p - k
        return Unit(self.i + q // self.U, q % self.U, self.U)

    def first(self, k):
        return isinstance(self.i, int) and self.n < k


def skewed(eng, count, stages, U=2, margin=2):
    lo, hi = min(s for s, _ in stages), max(s for s, _ in stages)
    begin = -(-(margin - lo) // U) * U
    end = (count - hi) // U * U

    def turn(i, p):
        for shift, stage in stages:
            q = p + shift
            u = Unit(i + q // U, q % U, U)
            if not isinstance(i, int) or 0 <= u.n < count:
                stage(u)

    if end - begin < 2 * U:
        begin = end = count - lo
    for t in range(-hi, begin):
        turn(t // U, t % U)
    if begin < end:
        with eng.Fori(begin // U, end // U) as i:
            for p in range(U):
                turn(i, p)
        for t in range(end, count - lo):
            turn(t // U, t % U)


class Norm:

    def __init__(self, sb, sem, name, K, mhalf, ready):
        self.K, self.mhalf, self.ready = K, mhalf, ready
        self.st = [sb(f"{name}_st{p}", [P, K, 6], F32) for p in range(2)]
        self.mv = [sb(f"{name}_mv{p}", [P, K, 2], F32) for p in range(2)]
        self.ve = [sb(f"{name}_ve{p}", [P, K], F32) for p in range(2)]
        self.rstd = [sb(f"{name}_rstd{p}", [P, K], F32) for p in range(2)]
        self.shift = [sb(f"{name}_shift{p}", [P, K], F32) for p in range(2)]
        self.bn, self.ag, self.vd = sem(f"{name}_bn"), sem(f"{name}_ag"), sem(f"{name}_var")
        self.pw, self.sh, self.done = sem(f"{name}_pow"), sem(f"{name}_shift"), sem(f"{name}_done")

    def stats(self, nc, dve, u, x):
        p = u.p % 2
        for k in range(self.K):
            last = nc.vector.bn_stats(self.st[p][:, k, :], x(k))
        last.then_inc(self.bn, 1)
        dve.wait_ge(self.bn, u.n + 1)
        if not u.first(2):
            dve.wait_ge(self.done, u.n - 1)
        dve.sem_inc(self.ready, 1)
        for k in range(self.K):
            last = nc.vector.bn_aggr(self.mv[p][:, k, :], self.st[p][:, k, :])
        last.then_inc(self.ag, 1)
        dve.wait_ge(self.ag, u.n + 1)
        nc.vector.tensor_scalar(self.ve[p][:, :], self.mv[p][:, :, 1], EPS, None, ALU.add).then_inc(self.vd, 1)

    def power(self, nc, pool, u):
        p = u.p % 2
        pool.wait_ge(self.vd, u.n + 1)
        if not u.first(2):
            pool.wait_ge(self.done, u.n - 1)
        nc.gpsimd.tensor_tensor(self.rstd[p][:, :], self.ve[p][:, :], self.mhalf[:, 0:self.K],
                                ALU.pow).then_inc(self.pw, 1)

    def offset(self, nc, dve, u):
        p = u.p % 2
        dve.wait_ge(self.pw, u.n + 1)
        nc.vector.scalar_tensor_tensor(self.shift[p][:, :], self.mv[p][:, :, 0], -1.0, self.rstd[p][:, :],
                                       ALU.mult, ALU.mult).then_inc(self.sh, 1)

    def apply(self, nc, act, u, x, out):
        p = u.p % 2
        act.wait_ge(self.sh, u.n + 1)
        for k in range(self.K):
            last = nc.scalar.activation(out(k), x(k), ACT.Relu, bias=self.shift[p][:, k:k + 1],
                                        scale=self.rstd[p][:, k:k + 1])
        last.then_inc(self.done, 1)


def build(nc, ins, out):
    x_in, adj_in, adjT_in, blocks_in, w_in = (ins[k] for k in ("x", "adj", "adjT", "blocks", "weights"))
    ctx = ExitStack()
    with ctx:
        def sem(name):
            return ctx.enter_context(nc.semaphore(name))

        def keep(name, shape, dt):
            return ctx.enter_context(nc.sbuf_tensor(name, shape, dt))

        bank = [ctx.enter_context(nc.psum_tensor(f"bank{i}", [P, W], F32)) for i in range(8)]

        X = keep("X", [P, B, P], F32)
        weights = keep("weights", [P, NCOL], F32)
        ident = keep("ident", [P, P], F32)
        ident_bf = keep("ident_bf", [P, P], BF16)
        mhalf = keep("mhalf", [P, 8], F32)

        def wt(name, a=0, b=None):
            lo, hi = COL[name]
            return weights[:, lo + a:(hi if b is None else lo + b)]

        layer0 = ExitStack()

        def sb(name, shape, dt):
            return layer0.enter_context(nc.sbuf_tensor(name, shape, dt))

        consts = sem("consts")
        past_dve, past_pool, past_sp = sem("past_dve"), sem("past_pool"), sem("past_sp")
        n0 = Norm(sb, sem, "n0", GROUP, mhalf, past_dve)
        adjT0 = [sb(f"adjT0_{p}", [P, GROUP, P], F32) for p in range(2)]
        h0n = [sb(f"h0n_{p}", [P, GROUP, P], F32) for p in range(2)]
        h0T = [sb(f"h0T_{p}", [P, GROUP, P], F32) for p in range(2)]
        a1rep = sb("a1rep", [P, P], F32)
        brep = sb("brep", [P, P], F32)
        a12 = sb("a12", [P, 1], F32)
        wa1 = sb("wa1", [P, P], F32)
        wplus = sb("wplus", [P, P + 1], F32)
        c0 = sb("c0", [P, 1], F32)
        v0 = [sb(f"v0_{p}", [P, GROUP, P + 1], F32) for p in range(2)]
        f0 = [sb(f"f0_{p}", [P, GROUP], F32) for p in range(2)]
        ex0 = [sb(f"ex0_{p}", [P, GROUP, P], F32) for p in range(2)]
        u0 = [sb(f"u0_{p}", [P, GROUP, P], F32) for p in range(2)]
        r0 = [sb(f"r0_{p}", [P, GROUP], F32) for p in range(2)]

        layer1 = ExitStack()

        def sb(name, shape, dt):
            return layer1.enter_context(nc.sbuf_tensor(name, shape, dt))

        n1 = Norm(sb, sem, "n1", PAIR, mhalf, past_dve)
        adj1 = [sb(f"adj1_{p}", [P, PAIR, P], F32) for p in range(2)]
        h1n = [sb(f"h1n_{p}", [P, PAIR, P], F32) for p in range(2)]
        h1T = [sb(f"h1T_{p}", [P, PAIR, P], F32) for p in range(2)]
        q_hi = [sb(f"q_hi_{p}", [P, PAIR, P], F32R) for p in range(2)]
        q_lo = [sb(f"q_lo_{p}", [P, PAIR, P], F32R) for p in range(2)]
        k_parts = [sb(f"k_parts_{p}", [P, 2, PAIR, P], F32R) for p in range(2)]
        k_diag = [sb(f"k_diag_{p}", [P, 2, PAIR, H, P], F32R) for p in range(2)]
        v1 = [sb(f"v1_{p}", [P, PAIR, H, SLOT], F32) for p in range(2)]
        edge = [sb(f"edge_{p}", [P, H, PAIR, P], F32) for p in range(2)]
        hide = [sb(f"hide_{p}", [P, PAIR, P], BF16) for p in range(2)]
        neg = [sb(f"neg_{p}", [P, HC, P], F32) for p in range(2)]
        nmax = [sb(f"nmax_{p}", [P, HC], F32) for p in range(2)]
        prob = [sb(f"prob_{p}", [P, HC, P], F32) for p in range(2)]
        probT = [sb(f"probT_{p}", [P, HC, P], F32) for p in range(2)]
        oT1 = [sb(f"oT1_{p}", [P, CH, P], F32) for p in range(2)]
        r1 = sb("r1", [P, PAIR * H], F32)
        o1 = [sb(f"o1_{p}", [P, PAIR * H, HD], F32) for p in range(2)]
        oc1 = [sb(f"oc1_{p}", [P, PAIR, P], F32) for p in range(2)]
        layer1.close()
        layer0.close()

        layer2 = ExitStack()

        def sb(name, shape, dt):
            return layer2.enter_context(nc.sbuf_tensor(name, shape, dt))

        T2 = 2 * TILES
        n2 = Norm(sb, sem, "n2", T2, mhalf, past_dve)
        x2 = [sb(f"x2_{p}", [P, T2, P], F32) for p in range(2)]
        a2 = [sb(f"a2_{p}", [P, T2, P], F32) for p in range(2)]
        normT = [sb(f"normT_{p}", [P, T2, P], F32) for p in range(2)]
        deg = [sb(f"deg_{p}", [P, T2], F32) for p in range(2)]
        degs = [sb(f"degs_{p}", [P, T2], F32) for p in range(2)]
        dpow = [sb(f"dpow_{p}", [P, T2], F32) for p in range(2)]
        dinv = [sb(f"dinv_{p}", [P, T2], F32) for p in range(2)]
        h2 = [sb(f"h2_{p}", [P, T2, P], F32) for p in range(2)]
        yT = sb("yT", [P, 2, W], F32)
        hidT = sb("hidT", [P, 2, 2, W], F32)
        s2T = sb("s2T", [P, 2, W], F32)
        s2 = sb("s2", [P, T2, P], F32)
        g2 = sb("g2", [P, 2, W], F32)
        f2 = sb("f2", [P, W], F32)
        f2a = sb("f2a", [P, W], F32)
        xn2 = [sb(f"xn2_{p}", [P, TILES, P], F32) for p in range(2)]
        fmax, fexp, fsum, frec, fw, fwb = (sb(n, [P, k], F32) for n, k in (
            ("fmax", 1), ("fexp", 5), ("fsum", 1), ("frec", 1), ("fw", 5), ("fwb", 5)))

        layer3 = ExitStack()

        def sb(name, shape, dt):
            return layer3.enter_context(nc.sbuf_tensor(name, shape, dt))

        def both(name, dt=F32, shape=(P, W)):
            return [sb(f"{name}_{s}", list(shape), dt) for s in range(2)]

        n3 = Norm(sb, sem, "n3", GROUP, mhalf, past_dve)
        adj3, edge3 = both("adj3"), both("edge3")
        start_n, start_T, state_T = both("start_n"), both("start_T"), both("state_T")
        state_n = both("state_n")
        h_hi, h_lo, agg_hi, agg_lo = (both(n, F32R) for n in ("h_hi", "h_lo", "agg_hi", "agg_lo"))
        reset, update, keep_, kept, cand, mixed = (both(n) for n in ("reset", "update", "keep", "kept", "cand", "mixed"))
        wc_hi, wc_lo = (sb(n, [P, LAYERS, GATES * P], F32R) for n in ("wc_hi", "wc_lo"))
        wh_hi, wh_lo = (sb(n, [P, GATES * P], F32R) for n in ("wh_hi", "wh_lo"))
        brz = sb("brz", [P, GATES], F32)
        layer3.close()
        layer2.close()

        def two(name):
            return [sem(f"{name}_{s}") for s in range(2)]

        in3, edge3d, flip0, flip3, natural3, flipE, split3 = (two(n) for n in (
            "in3", "edge3_done", "start_transposed", "state_transposed", "state_n_done", "end_transposed", "split_done"))
        startS, x3 = two("start_hi_done"), two("x3_done")
        aggP, aggH, aggL, gateR, gateZ, gateN, resetD, updateD, dotD, preD, candD, keepD, keptD, mixD, stateD, hiD = (
            sem(n) for n in ("agg_product", "agg_hi_done", "agg_lo_done", "reset_ready", "update_ready", "cand_ready",
                             "reset_done", "update_done", "reset_dot_done", "pre_done", "cand_done", "keep_done",
                             "kept_done", "mix_done", "state_done", "h_hi_done"))

        def nth(count, s):
            return 2 * count + s - 1

        wcP, wcH, wcD, whD = (sem(n) for n in ("wc_product", "wc_hi_done", "wc_done", "wh_done"))

        in_x2 = [sem(f"in_x2_{p}") for p in range(2)]
        in_a2 = [sem(f"in_a2_{p}") for p in range(2)]
        clear2, soft2, soft2s, plus2, degD, degp, dinvD, rows2, flip2, normD = (sem(s) for s in (
            "clear2", "soft2", "soft2_exp", "plus2", "deg_done", "deg_power", "dinv_done", "rows2", "flip2", "normT_done"))
        y2, y2d, hid2, hid2d, s2p, s2d, t2, t2d, o2, o2d, f2d, b2, x2d = (sem(s) for s in (
            "y2", "y2_done", "hid2", "hid2_done", "s2T_product", "s2T_done", "s2_transposed", "s2_done", "o2",
            "g2_done", "f2_done", "back2", "xn2_done"))
        out2 = [sem(f"x2_written_{p}") for p in range(2)]

        w_first, w_rest = sem("w_first"), sem("w_rest")
        in1 = [sem(f"in1_{p}") for p in range(2)]
        in_k = [sem(f"in_k_{p}") for p in range(2)]
        clear1, hideD, edgeD = sem("clear1"), sem("hide_done"), sem("edge_done")
        t1, hT1, qk1, hi1, lo1, vp1, vd1 = (sem(s) for s in (
            "t1_done", "hT1_done", "qk1_product", "hi1_done", "lo1_done", "v1_product", "v1_done"))
        score, shifted, probD, flip, flipped, pv, flippedS = (sem(s) for s in (
            "scores_ready", "shifted_ready", "probs_ready", "probs_transposed", "probT_ready", "pv_done", "last_probT_ready"))
        oT1d, back1, rd1, o1d, tc1, oc1d, wo1, x1 = (sem(s) for s in (
            "oT1_done", "back1_done", "r1_done", "o1_done", "oc1_product", "oc1_done", "wo1_done", "x1_done"))
        in_x = [sem(f"in_x_{p}") for p in range(2)]
        in_adjT = [sem(f"in_adjT_{p}") for p in range(2)]
        pre0, prod0, fold0 = sem("pre0"), sem("prod0"), sem("fold0")
        t0, hT0, e0, v0p, v0d, fd0, exd0, ud0, o0, rd0, x0 = (sem(s) for s in (
            "t0_done", "hT0_done", "e0_done", "v0_product", "v0_done", "f0_done", "exp0_done", "u0_done",
            "o0_done", "r0_done", "x0_done"))
        x_out = sem("x_out")

        def halves(lo):
            return [bank[lo + b][:, 0:2 * (P + 1)].rearrange("p (g c) -> p g c", g=2) for b in range(2)]

        def rows_of(a):
            return a.rearrange("p (g s) -> p g s", s=SLOT)

        def slots(a, g):
            if g == 0:
                return rows_of(a)[:, :, 0:NN]
            if len(SPANS[g]) == 1:
                return rows_of(a)[:, :, slice(*SPANS[g][0])]
            (lo, mid), (nxt, _) = SPANS[g]
            return rows_of(a)[:, :, 16:28].rearrange("p g (s k) -> p g s k", k=3)[:, :, (lo - 16) // 3::2, :]

        block = ctx.enter_context(nc.Block())

        @block.sync
        def _(sp):
            sp.dma_start(weights[:, 0:FIRST], w_in[:, 0:FIRST]).then_inc(w_first, 16)

            def load_x(u):
                if not u.first(2):
                    sp.wait_ge(n0.bn, u.n - 1)
                sp.sem_inc(past_sp, 1)
                sp.dma_start(X[:, bass.ds(u.n * GROUP, GROUP), :],
                             x_in[:, bass.ds(u.n * GROUP, GROUP), :]).then_inc(in_x[u.p], 16)

            def load_adjT(u):
                if not u.first(2):
                    sp.wait_ge(ud0, u.n - 1)
                sp.sem_inc(past_sp, 1)
                sp.dma_start(adjT0[u.p][:, :, :],
                             adjT_in[:, bass.ds(u.n * GROUP, GROUP), :]).then_inc(in_adjT[u.p], 16)
                if u.first(1):
                    sp.dma_start(weights[:, FIRST:NCOL], w_in[:, FIRST:NCOL]).then_inc(w_rest, 16)

            skewed(sp, NG, [(2, load_x), (0, load_adjT)])

            def load_adj1(u):
                if not u.first(2):
                    sp.wait_ge(edgeD, u.n - 1)
                    sp.wait_ge(hideD, u.n - 1)
                sp.sem_inc(past_sp, 1)
                sp.dma_start(adj1[u.p][:, :, :], adj_in[:, bass.ds(u.n * PAIR, PAIR), :]).then_inc(in1[u.p], 16)

            def spread_k(u):
                p = u.p
                sp.wait_ge(lo1, u.n + 1)
                sp.sem_inc(past_sp, 1)
                if u.first(1):
                    sp.wait_ge(clear1, 1)
                if not u.first(2):
                    sp.wait_ge(score, CH * (u.n - 1))
                sp.sem_inc(past_sp, 1)
                for h in range(H):
                    rows = slice(HD * h, HD * (h + 1))
                    sp.dma_start(k_diag[p][rows, :, :, h, :].bitcast(F32), k_parts[p][rows, :, :, :].bitcast(F32)).then_inc(in_k[p], 16)

            skewed(sp, NP, [(1, spread_k), (2, load_adj1)])

            sp.wait_ge(x1, NP)
            sp.wait_ge(clear2, 1)

            def gather2(u):
                p, g0 = u.p, BG * u.n
                if not u.first(2):
                    sp.wait_ge(x2d, u.n - 1)
                    sp.wait_ge(rows2, u.n - 1)
                    sp.wait_ge(flip2, 2 * (u.n - 1))
                sp.sem_inc(past_sp, 1)
                sp.dma_start(a2[p][:, :, :], blocks_in[:, u.n, :, :, :].rearrange("p l t c -> p (l t) c")).then_inc(in_a2[p], 16)
                for s in range(4):
                    graphs = slice(g0 + s, g0 + BG, 4)
                    sp.dma_start(x2[p][SLOT * s:SLOT * s + NN, 0:TILES, :], X[0:NN, graphs, :]).then_inc(in_x2[p], 16)
                    for row, node, count in RUNS:
                        sp.dma_start(x2[p][SLOT * s + row:SLOT * s + row + count, TILES:T2, :],
                                     X[node:node + count, graphs, :]).then_inc(in_x2[p], 16)

            def scatter2(u):
                p, g0 = u.p, BG * u.n
                sp.wait_ge(x2d, u.n + 1)
                for s in range(4):
                    sp.dma_start(X[0:NN, slice(g0 + s, g0 + BG, 4), :], xn2[p][SLOT * s:SLOT * s + NN, :, :]).then_inc(out2[p], 16)

            skewed(sp, NB, [(1, gather2), (0, scatter2)])

            sp.wait_ge(x2d, NB)

            def load3(i, s):
                if isinstance(i, int) and i == 0:
                    pass
                else:
                    sp.wait_ge(edge3d[s], i)
                    sp.sem_inc(past_sp, 1)
                sp.dma_start(adj3[s][:, :], adj_in[:, bass.ds((2 * i + s) * GROUP, GROUP), :].rearrange("p g n -> p (g n)")
                             ).then_inc(in3[s], 16)

            def store3(i, s):
                sp.wait_ge(x3[s], i + 1)
                sp.sem_inc(past_sp, 1)
                rows = bass.ds((2 * i + s) * GROUP, GROUP)
                sp.dma_start(out[:, rows, :], X[:, rows, :]).then_inc(x_out, 16)

            for s in range(2):
                load3(0, s)
            with sp.Fori(1, NG // 2) as i:
                for s in range(2):
                    load3(i, s)
                for s in range(2):
                    store3(i - 1, s)
            for s in range(2):
                store3(NG // 2 - 1, s)
            sp.wait_ge(x_out, 16 * NG)

        @block.gpsimd
        def _(pool):
            nc.gpsimd.memset(mhalf[:, :], -0.5)
            nc.gpsimd.memset(ident[:, :], 1.0).then_inc(consts, 1)
            pool.wait_ge(consts, 1)
            nc.gpsimd.affine_select(out=ident[:, :], in_=ident[:, :], compare_op=ALU.is_equal, fill=0.0, base=0,
                                    pattern=[[-1, P]], channel_multiplier=1).then_inc(consts, 1)
            pool.wait_ge(consts, 2)
            nc.gpsimd.tensor_copy(ident_bf[:, :], ident[:, :])
            for p in range(2):
                last = nc.gpsimd.memset(v0[p][:, :, P:P + 1], 1.0)
            last.then_inc(consts, 1)

            def u_product(u):
                p = u.p
                pool.wait_ge(exd0, u.n + 1)
                pool.wait_ge(in_adjT[p], 16 * (u.i + 1))
                if not u.first(2):
                    pool.wait_ge(o0, u.n - 1)
                nc.gpsimd.tensor_tensor(u0[p][:, :, :], ex0[p][:, :, :], adjT0[p][:, :, :], ALU.mult).then_inc(ud0, 1)

            def power0(u):
                n0.power(nc, pool, u)

            for p in range(2):
                nc.gpsimd.memset(k_diag[p][:, :, :, :, :].bitcast(F32), 0.0)
                nc.gpsimd.memset(v1[p][:, :, :, HD + 1:SLOT], 0.0)
                last = nc.gpsimd.memset(v1[p][:, :, :, HD:HD + 1], 1.0)
            last.then_inc(clear1, 1)
            skewed(pool, NG, [(2, power0), (0, u_product)])

            def power1(u):
                n1.power(nc, pool, u)

            def edges(u):
                p = u.p
                if u.first(1):
                    pool.wait_ge(w_rest, 16)
                if not u.first(2):
                    pool.wait_ge(shifted, CH * (u.n - 1))
                pool.wait_ge(in1[p], 16 * (u.i + 1))
                pool.sem_inc(past_pool, 1)
                for h in range(H):
                    last = nc.gpsimd.tensor_scalar(edge[p][:, h, :, :], adj1[p][:, :, :], wt("we", h, h + 1), 0.0,
                                                   ALU.mult, ALU.add)
                last.then_inc(edgeD, 1)

            skewed(pool, NP, [(1, edges), (3, power1)])

            pool.wait_ge(x1, NP)
            for p in range(2):
                nc.gpsimd.memset(x2[p][:, :, :], 0.0)
            nc.gpsimd.memset(s2T[:, :, :], 0.0)
            nc.gpsimd.memset(f2[:, :], 0.0).then_inc(clear2, 1)

            def power_deg(u):
                p = u.p
                pool.wait_ge(degD, u.n + 1)
                nc.gpsimd.tensor_tensor(dpow[p][:, :], degs[p][:, :], mhalf[:, 0:T2], ALU.pow).then_inc(degp, 1)

            def power2(u):
                n2.power(nc, pool, u)

            skewed(pool, NB, [(1, power_deg), (1, power2)])

            pool.wait_ge(x2d, NB)

            def power3(i, s):
                n3.power(nc, pool, Unit(i, s))

            def keep3(i, l, s):
                c = LAYERS * i + l
                pool.wait_ge(updateD, nth(c + 1, s))
                pool.sem_inc(past_pool, 1)
                nc.gpsimd.tensor_scalar(keep_[s][:, :], update[s][:, :], -1.0, 1.0, ALU.mult, ALU.add).then_inc(keepD, 1)
                nc.gpsimd.tensor_tensor(kept[s][:, :], update[s][:, :], (start_T if l == 0 else state_T)[s][:, :],
                                        ALU.mult).then_inc(keptD, 1)

            for s in range(2):
                power3(0, s)

            def turns3(i, last=False):
                for l in range(LAYERS):
                    for s in range(2):
                        keep3(i, l, s)
                        if l == 1 and not last:
                            power3(i + 1, s)

            turns3(0)
            with pool.Fori(1, NG // 2 - 1) as i:
                turns3(i)
            turns3(NG // 2 - 1, last=True)

        @block.scalar
        def _(act):
            def apply0(u):
                p = u.p
                if not u.first(2):
                    act.wait_ge(t0, u.n - 1)
                n0.apply(nc, act, u, lambda k: X[:, u.n * GROUP + k, :], lambda k: h0n[p][:, k, :])

            def evac_hT(u):
                p = u.p
                act.wait_ge(t0, u.n + 1)
                if not u.first(2):
                    act.wait_ge(v0p, u.n - 1)
                nc.scalar.activation(h0T[p][:, :, :], bank[p][:, :], ACT.Copy).then_inc(hT0, 1)

            def exp0(u):
                p = u.p
                act.wait_ge(e0, u.n + 1)
                act.wait_ge(fd0, u.n + 1)
                if not u.first(2):
                    act.wait_ge(ud0, u.n - 1)
                for k in range(GROUP):
                    last = nc.scalar.activation(ex0[p][:, k, :], bank[2 + p][:, k * P:(k + 1) * P], ACT.Exp,
                                                bias=f0[p][:, k:k + 1])
                last.then_inc(exd0, 1)

            skewed(act, NG, [(1, apply0), (0, exp0), (1, evac_hT)])

            def apply1(u):
                p = u.p
                if not u.first(2):
                    act.wait_ge(t1, u.n - 1)
                n1.apply(nc, act, u, lambda k: X[:, u.n * PAIR + k, :], lambda k: h1n[p][:, k, :])

            def copy_hT1(u):
                p = u.p
                act.wait_ge(t1, u.n + 1)
                if not u.first(2):
                    act.wait_ge(vp1, u.n - 1)
                nc.scalar.activation(h1T[p][:, :, :], bank[4][:, 0:PAIR * P], ACT.Copy).then_inc(hT1, 1)

            def qk_hi(u):
                p = u.p
                act.wait_ge(qk1, u.n + 1)
                if not u.first(2):
                    act.wait_ge(score, CH * (u.n - 1))
                    act.wait_ge(in_k[p], H * 16 * u.i)
                nc.scalar.activation(q_hi[p][:, :, :], bank[5][:, 0:PAIR * P], ACT.Copy, scale=HD ** -0.5)
                nc.scalar.activation(k_parts[p][:, 0, :, :], bank[5][:, PAIR * P:2 * PAIR * P], ACT.Copy).then_inc(hi1, 1)

            def copy_v(u):
                p = u.p
                act.wait_ge(vp1, u.n + 1)
                if u.first(1):
                    act.wait_ge(clear1, 1)
                if not u.first(2):
                    act.wait_ge(pv, CH * (u.n - 1))
                nc.scalar.activation(v1[p][:, :, :, 0:HD],
                                     bank[4][:, PAIR * P:2 * PAIR * P].rearrange("p (g h d) -> p g h d", g=PAIR, h=H),
                                     ACT.Copy).then_inc(vd1, 1)

            def exps(j):
                def stage(u):
                    p = j % 2
                    act.wait_ge(shifted, CH * u.n + j + 1)
                    if not (u.first(1) and j < 2):
                        act.wait_ge(flip, CH * u.n + j - 1)
                    for h in range(HC):
                        last = nc.scalar.activation(prob[p][:, h, :], neg[p][:, h, :], ACT.Exp,
                                                    bias=nmax[p][:, h:h + 1], scale=-1.0)
                    last.then_inc(probD, 1)
                return stage

            def copy_last_probT(u):
                j = CH - 1
                act.wait_ge(flip, CH * u.n + j + 1)
                act.wait_ge(pv, CH * u.n + j - 1)
                nc.scalar.activation(probT[j % 2][:, :, :], bank[2 + j % 2][:, :], ACT.Copy).then_inc(flippedS, 1)

            def copy_oT1(u):
                p = u.p
                act.wait_ge(pv, CH * (u.n + 1))
                if not u.first(2):
                    act.wait_ge(back1, u.n - 1)
                nc.scalar.activation(oT1[p][:, :, :], bank[6][:, :], ACT.Copy).then_inc(oT1d, 1)

            def copy_oc1(u):
                p = u.p
                act.wait_ge(tc1, u.n + 1)
                if not u.first(2):
                    act.wait_ge(wo1, u.n - 1)
                nc.scalar.activation(oc1[p][:, :, :], bank[7][:, 0:PAIR * P], ACT.Copy).then_inc(oc1d, 1)

            skewed(act, NP, [(1, qk_hi), (0, exps(1)), (-1, copy_oT1), (0, exps(2)), (1, copy_v), (2, apply1),
                             (0, exps(3)), (-1, copy_oc1), (1, exps(0)), (0, copy_last_probT), (2, copy_hT1)])

            act.wait_ge(soft2, 1)
            nc.scalar.activation(fexp[:, :], wt("fw"), ACT.Exp, bias=fmax[:, :], accum_out=fsum[:, :]).then_inc(soft2s, 1)

            def apply2(u):
                p = u.p
                if not u.first(2):
                    act.wait_ge(y2, 2 * (u.n - 1))
                n2.apply(nc, act, u, lambda k: x2[p][:, k, :], lambda k: h2[p][:, k, :])

            def scale_columns(u):
                p = u.p
                for l in range(2):
                    act.wait_ge(flip2, 2 * u.n + l + 1)
                    if l == 0 and not u.first(2):
                        act.wait_ge(o2, 2 * (u.n - 1))
                    for k in range(TILES):
                        t = TILES * l + k
                        last = nc.scalar.activation(normT[p][:, t, :], bank[0][:, k * P:(k + 1) * P], ACT.Copy,
                                                    scale=dinv[p][:, t:t + 1])
                    last.then_inc(normD, 1)

            def hidden2(u):
                for l in range(2):
                    for half in range(2):
                        act.wait_ge(hid2, 4 * u.n + 2 * l + half + 1)
                        if l == half == 0 and not u.first(1):
                            act.wait_ge(s2p, 2 * u.n)
                        for g in (range(1) if l == 0 else range(1, 5)):
                            last = nc.scalar.activation(slots(hidT[:, half, l, :], g), slots(bank[3 + 2 * l + half][:, :], g), ACT.Relu,
                                                        bias=wt("b1", 2 * g + half, 2 * g + half + 1))
                        last.then_inc(hid2d, 1)

            def outputs2(u):
                for l in range(2):
                    act.wait_ge(o2, 2 * u.n + l + 1)
                    if u.first(1):
                        act.wait_ge(soft2, 3)
                    else:
                        act.wait_ge(f2d, 3 * u.n)
                    for g in (range(1) if l == 0 else range(1, 5)):
                        last = nc.scalar.activation(slots(g2[:, l, :], g), slots(bank[5 + l][:, :], g), ACT.Relu,
                                                    bias=fwb[:, g:g + 1], scale=fw[:, g:g + 1])
                    last.then_inc(o2d, 1)

            skewed(act, NB, [(1, apply2), (1, scale_columns), (0, hidden2), (0, outputs2)])

            for l in range(LAYERS):
                act.wait_ge(wcP, l + 1)
                nc.scalar.activation(wc_hi[:, l, :], bank[l][:, 0:GATES * P], ACT.Copy).then_inc(wcH, 1)

            def apply3(i, s):
                u = Unit(i, s)
                if not u.first(2):
                    act.wait_ge(aggP, nth(LAYERS * (i - 1) + 1, s))
                    act.wait_ge(flip0[s], i)
                n3.apply(nc, act, u, lambda k: X[:, u.n * GROUP + k, :], lambda k: start_n[s][:, k * P:(k + 1) * P])

            def start_hi(i, s):
                act.wait_ge(flip0[s], i + 1)
                if not (isinstance(i, int) and i == 0):
                    act.wait_ge(gateN, nth(LAYERS * i, s))
                nc.scalar.activation(h_hi[s][:, :], bank[4 * s + 3][:, :], ACT.Copy).then_inc(startS[s], 1)

            def copy_state_n(i, l, s):
                act.wait_ge(flip3[s], (LAYERS - 1) * i + l)
                nc.scalar.activation(state_n[s][:, :], bank[4 * s + 3][:, :], ACT.Copy).then_inc(natural3[s], 1)

            def agg_upper(i, l, s):
                act.wait_ge(aggP, nth(LAYERS * i + l + 1, s))
                nc.scalar.activation(agg_hi[s][:, :], bank[4 * s + 2][:, :], ACT.Copy).then_inc(aggH, 1)

            def gate(i, l, s, b, ready, done, to):
                act.wait_ge(ready, nth(LAYERS * i + l + 1, s))
                nc.scalar.activation(to[s][:, :], bank[4 * s + b][:, :], ACT.Sigmoid, bias=brz[:, b:b + 1]).then_inc(done, 1)

            def candidate(i, l, s):
                act.wait_ge(preD, nth(LAYERS * i + l + 1, s))
                nc.scalar.activation(cand[s][:, :], cand[s][:, :], ACT.Tanh, bias=wt("bih", 2, 3)).then_inc(candD, 1)

            def turns3(i, first=False, last=False):
                for l in range(LAYERS):
                    for s in range(2):
                        post = (i, l, 0) if s else (i, l - 1, 1) if l else (i - 1, LAYERS - 1, 1)
                        busy = not (first and l == s == 0)
                        if busy:
                            gate(*post, 0, gateR, resetD, reset)
                        if l:
                            copy_state_n(i, l, s)
                        if busy:
                            gate(*post, 1, gateZ, updateD, update)
                            candidate(*post)
                        agg_upper(i, l, s)
                        if l == 3 and not last:
                            apply3(i + 1, s)
                        if l == 4 and s == 1 and not last:
                            start_hi(i + 1, 0)
                        if l == 0 and s == 0:
                            start_hi(i, 1)

            act.wait_ge(whD, 2)
            for s in range(2):
                apply3(0, s)
            start_hi(0, 0)
            turns3(0, first=True)
            with act.Fori(1, NG // 2 - 1) as i:
                turns3(i)
            turns3(NG // 2 - 1, last=True)
            post = (NG // 2 - 1, LAYERS - 1, 1)
            gate(*post, 0, gateR, resetD, reset)
            gate(*post, 1, gateZ, updateD, update)
            candidate(*post)

        @block.tensor
        def _(pe):
            pe.wait_ge(w_first, 16)
            pe.wait_ge(pre0, 3)
            pe.matmul(bank[4][:, 0:P], wt("ww"), a1rep[:, :], start=True, stop=True)
            pe.matmul(bank[4][:, P:P + 1], wt("ww"), wt("acol", 1, 2), start=True, stop=True)
            pe.matmul(bank[4][:, P + 1:P + 2], brep[:, :], a12[:, :], start=True, stop=True).then_inc(prod0, 1)
            pe.wait_ge(consts, 3)

            def transpose_h(u):
                p = u.p
                pe.wait_ge(n0.done, u.n + 1)
                if not u.first(2):
                    pe.wait_ge(hT0, u.n - 1)
                for k in range(GROUP):
                    last = pe.transpose(bank[p][:, k * P:(k + 1) * P], h0n[p][:, k, :], ident[:, :])
                last.then_inc(t0, 1)

            def logits(u):
                p = u.p
                pe.wait_ge(hT0, u.n + 1)
                if u.first(1):
                    pe.wait_ge(fold0, 3)
                if not u.first(2):
                    pe.wait_ge(exd0, u.n - 1)
                pe.matmul(bank[2 + p][:, :], wa1[:, :], h0T[p][:, :, :], start=True, stop=True).then_inc(e0, 1)

            def values(u):
                p = u.p
                if not u.first(1):
                    pe.wait_ge(v0d, u.n)
                    pe.wait_ge(fd0, u.n)
                for k in range(GROUP):
                    last = pe.matmul(halves(4)[k // 2][:, k % 2, :], h0T[p][:, k, :], wplus[:, :],
                                     start=True, stop=True)
                last.then_inc(v0p, 1)

            def attend(u):
                p = u.p
                pe.wait_ge(ud0, u.n + 1)
                pe.wait_ge(v0d, u.n + 1)
                if not u.first(1):
                    pe.wait_ge(x0, u.n)
                for k in range(GROUP):
                    last = pe.matmul(halves(6)[k // 2][:, k % 2, :], u0[p][:, k, :], v0[p][:, k, :],
                                     start=True, stop=True)
                last.then_inc(o0, 1)

            skewed(pe, NG, [(1, transpose_h), (0, logits), (0, values), (-1, attend)])

            pe.wait_ge(x0, NG)
            pe.wait_ge(w_rest, 16)

            def transpose_h1(u):
                p = u.p
                pe.wait_ge(n1.done, u.n + 1)
                if not u.first(1):
                    pe.wait_ge(vd1, u.n)
                for k in range(PAIR):
                    last = pe.transpose(bank[4][:, k * P:(k + 1) * P], h1n[p][:, k, :], ident[:, :])
                last.then_inc(t1, 1)

            def project_qk(u):
                p = u.p
                pe.wait_ge(hT1, u.n + 1)
                if not u.first(1):
                    pe.wait_ge(lo1, u.n)
                pe.matmul(bank[5][:, 0:PAIR * P], wt("wqT"), h1T[p][:, :, :], start=True, stop=True)
                pe.matmul(bank[5][:, PAIR * P:2 * PAIR * P], wt("wkT"), h1T[p][:, :, :], start=True, stop=True).then_inc(qk1, 1)

            def project_v(u):
                p = u.p
                for k in range(PAIR):
                    last = pe.matmul(bank[4][:, (PAIR + k) * P:(PAIR + k + 1) * P], h1T[p][:, k, :], wt("wvT"),
                                     start=True, stop=True)
                last.then_inc(vp1, 1)

            def scores(j):
                def stage(u):
                    p, g, c = u.p, j // 2, j % 2
                    to = bank[j % 2][:, :].rearrange("p (h n) -> p h n", h=HC)
                    if j == 0:
                        pe.wait_ge(hideD, u.n + 1)
                        pe.wait_ge(in_k[p], H * 16 * (u.i + 1))
                    if not (u.first(1) and j < 2):
                        pe.wait_ge(shifted, CH * u.n + j - 1)
                    heads = slice(HC * c, HC * (c + 1))
                    pe.matmul(to, ident_bf[:, :], hide[p][:, g, :].unsqueeze(1).broadcast_to([P, HC, P]), start=True, stop=False)
                    pe.matmul(to, q_hi[p][:, g, :], k_diag[p][:, 0, g, heads, :], start=False, stop=False)
                    pe.matmul(to, q_hi[p][:, g, :], k_diag[p][:, 1, g, heads, :], start=False, stop=False)
                    pe.matmul(to, q_lo[p][:, g, :], k_diag[p][:, 0, g, heads, :], start=False, stop=True).then_inc(score, 1)
                return stage

            def copied(u, j):
                if j == CH - 1:
                    pe.wait_ge(flippedS, u.n + 1)
                else:
                    pe.wait_ge(flipped, (CH - 1) * u.n + j + 1)

            def transpose_probs(j):
                def stage(u):
                    pe.wait_ge(probD, CH * u.n + j + 1)
                    if j >= 2:
                        pe.wait_ge(flipped, (CH - 1) * u.n + j - 1)
                    elif not u.first(1):
                        copied(u.back(1), j + 2)
                    for h in range(HC):
                        last = pe.transpose(bank[2 + j % 2][:, h * P:(h + 1) * P], prob[j % 2][:, h, :], ident[:, :])
                    last.then_inc(flip, 1)
                return stage

            def weigh_values(j):
                def stage(u):
                    p, g, c = u.p, j // 2, j % 2
                    copied(u, j)
                    if j == 0:
                        pe.wait_ge(vd1, u.n + 1)
                        if not u.first(1):
                            pe.wait_ge(oT1d, u.n)
                    for h in range(HC):
                        last = pe.matmul(bank[6][SLOT * h:SLOT * (h + 1), j * P:(j + 1) * P],
                                         v1[p][:, g, HC * c + h, :], probT[j % 2][:, h, :], start=True, stop=True)
                    last.then_inc(pv, 1)
                return stage

            def turn_back(u):
                p = u.p
                pe.wait_ge(oT1d, u.n + 1)
                if not u.first(1):
                    pe.wait_ge(x1, u.n)
                for j in range(CH):
                    last = pe.transpose(bank[7][:, j * P:(j + 1) * P], oT1[p][:, j, :], ident[:, :])
                last.then_inc(back1, 1)

            def transpose_o(u):
                p = u.p
                pe.wait_ge(o1d, u.n + 1)
                for k in range(PAIR):
                    last = pe.transpose(bank[7][:, k * P:(k + 1) * P],
                                        o1[p][:, k * H:(k + 1) * H, :].rearrange("p h d -> p (h d)"), ident[:, :])
                last.then_inc(tc1, 1)

            def project_o(u):
                p = u.p
                pe.wait_ge(oc1d, u.n + 1)
                for k in range(PAIR):
                    last = pe.matmul(bank[7][:, k * P:(k + 1) * P], oc1[p][:, k, :], wt("woT"), start=True, stop=True)
                last.then_inc(wo1, 1)

            skewed(pe, NP, [(1, project_qk), (0, scores(2)), (0, transpose_probs(0)), (-1, weigh_values(3)),
                            (1, project_v), (0, scores(3)), (0, transpose_probs(1)), (0, weigh_values(0)), (-1, turn_back),
                            (1, scores(0)), (0, transpose_probs(2)), (0, weigh_values(1)), (-1, transpose_o),
                            (1, scores(1)), (0, transpose_probs(3)), (0, weigh_values(2)), (-1, project_o),
                            (2, transpose_h1)])

            def transpose_norm(u):
                p = u.p
                for l in range(2):
                    pe.wait_ge(rows2, u.n + 1)
                    if l == 1 or not u.first(1):
                        pe.wait_ge(normD, 2 * u.n + l)
                    for k in range(TILES):
                        last = pe.transpose(bank[0][:, k * P:(k + 1) * P], a2[p][:, TILES * l + k, :], ident[:, :])
                    last.then_inc(flip2, 1)

            def aggregate2(u):
                p = u.p
                pe.wait_ge(n2.done, u.n + 1)
                for l in range(2):
                    pe.wait_ge(normD, 2 * u.n + l + 1)
                    if not u.first(1):
                        pe.wait_ge(s2d, 2 * u.n - 1 + l)
                    for k in range(TILES):
                        t = TILES * l + k
                        last = pe.matmul(bank[1 + l][:, k * P:(k + 1) * P], h2[p][:, t, :], normT[p][:, t, :], start=True, stop=True)
                    last.then_inc(y2, 1)

            def hidden_product(u):
                for l in range(2):
                    pe.wait_ge(y2d, 2 * u.n + l + 1)
                    for half in range(2):
                        if not u.first(1):
                            pe.wait_ge(t2d if l == 0 else o2d, 2 * u.n - 1 + half)
                        for g in (range(1) if l == 0 else range(1, 5)):
                            at = g * HID + half * P
                            last = pe.matmul(slots(bank[3 + 2 * l + half][:, :], g), wt("w1", at, at + P), slots(yT[:, l, :], g),
                                             start=True, stop=True)
                        last.then_inc(hid2, 1)

            def output_product(u):
                for l in range(2):
                    pe.wait_ge(hid2d, 4 * u.n + 2 * l + 2)
                    pe.wait_ge(y2d, 2 * u.n + l + 1)
                    for g in (range(1) if l == 0 else range(1, 5)):
                        for half in range(2):
                            at = (2 * g + half) * P
                            last = pe.matmul(slots(bank[1 + l][:, :], g), wt("w2", at, at + P), slots(hidT[:, half, l, :], g),
                                             start=(half == 0), stop=(half == 1))
                    last.then_inc(s2p, 1)

            def transpose_s2(u):
                for l in range(2):
                    pe.wait_ge(s2d, 2 * u.n + l + 1)
                    for k in range(TILES):
                        last = pe.transpose(bank[3 + l][:, k * P:(k + 1) * P], s2T[:, l, k * P:(k + 1) * P], ident[:, :])
                    last.then_inc(t2, 1)

            def aggregate_out(u):
                p = u.p
                for l in range(2):
                    pe.wait_ge(t2d, 2 * u.n + l + 1)
                    pe.wait_ge(hid2d, 4 * u.n + 4)
                    for k in range(TILES):
                        t = TILES * l + k
                        last = pe.matmul(bank[5 + l][:, k * P:(k + 1) * P], s2[:, t, :], normT[p][:, t, :], start=True, stop=True)
                    last.then_inc(o2, 1)

            def back_rows(u):
                pe.wait_ge(f2d, 3 * (u.n + 1))
                if not u.first(1):
                    pe.wait_ge(x2d, u.n)
                for k in range(TILES):
                    last = pe.transpose(bank[7][:, k * P:(k + 1) * P], f2[:, k * P:(k + 1) * P], ident[:, :])
                last.then_inc(b2, 1)

            pe.wait_ge(x1, NP)
            skewed(pe, NB, [(1, transpose_norm), (0, aggregate2), (0, hidden_product), (0, output_product), (0, transpose_s2),
                            (0, aggregate_out), (0, back_rows)])

            pe.wait_ge(x2d, NB)
            for l in range(LAYERS):
                pe.matmul(bank[l][:, 0:GATES * P], wt("gwT", l * P, (l + 1) * P), wt("wihT"), start=True, stop=True).then_inc(wcP, 1)

            def transpose_start(i, s):
                pe.wait_ge(n3.done, 2 * i + s + 1)
                if not (isinstance(i, int) and i == 0):
                    pe.wait_ge(dotD, nth(LAYERS * i, s))
                for k in range(GROUP):
                    last = pe.transpose(bank[4 * s + 3][:, k * P:(k + 1) * P], start_n[s][:, k * P:(k + 1) * P], ident[:, :])
                last.then_inc(flip0[s], 1)

            def transpose_state(to, s, done):
                for k in range(GROUP):
                    last = pe.transpose(to[:, k * P:(k + 1) * P], state_T[s][:, k * P:(k + 1) * P], ident[:, :])
                last.then_inc(done[s], 1)

            def transpose_end(i, s, more=True):
                pe.wait_ge(stateD, nth(LAYERS * (i + 1), s))
                if more:
                    pe.wait_ge(split3[s], LAYERS * (i + 1) + 1)
                transpose_state(bank[4 * s + 3], s, flipE)

            def recurrent(s, q):
                to = bank[4 * s + (q if q < 2 else 3)][:, :]
                cols = slice(q * P, (q + 1) * P)
                pe.matmul(to, wh_hi[:, cols], h_hi[s][:, :], start=True, stop=False)
                pe.matmul(to, wh_lo[:, cols], h_hi[s][:, :], start=False, stop=False)
                return pe.matmul(to, wh_hi[:, cols], h_lo[s][:, :], start=False, stop=(q == 2))

            def turns3(i, first=False, last=False):
                for l in range(LAYERS):
                    for s in range(2):
                        c = LAYERS * i + l
                        if l:
                            pe.wait_ge(stateD, nth(c, s))
                            transpose_state(bank[4 * s + 3], s, flip3)
                        elif not first:
                            transpose_end(i - 1, s)
                        pe.wait_ge(split3[s], c + 1)
                        recurrent(s, 0)
                        recurrent(s, 1)
                        if l == 0 and s == 0:
                            transpose_start(i, 1)
                        if l == 4 and s == 1 and not last:
                            transpose_start(i + 1, 0)
                        if l:
                            pe.wait_ge(natural3[s], (LAYERS - 1) * i + l)
                        else:
                            pe.wait_ge(edge3d[s], i + 1)
                        state = (state_n if l else start_n)[s]
                        for k in range(GROUP):
                            cols = slice(k * P, (k + 1) * P)
                            mm = pe.matmul(bank[4 * s + 2][:, cols], state[:, cols], edge3[s][:, cols], start=True, stop=True)
                        mm.then_inc(aggP, 1)
                        if l == 0 and not first:
                            pe.wait_ge(x3[s], i)
                        recurrent(s, 2)
                        pe.wait_ge(aggH, nth(c + 1, s))
                        for q in range(GATES):
                            to = bank[4 * s + q][:, :]
                            cols = slice(q * P, (q + 1) * P)
                            if q == 2:
                                pe.wait_ge(aggL, nth(c + 1, s))
                            pe.matmul(to, wc_hi[:, l, cols], agg_hi[s][:, :], start=(q == 2), stop=False)
                            pe.matmul(to, wc_lo[:, l, cols], agg_hi[s][:, :], start=False, stop=False)
                        for q, ready in enumerate((gateR, gateZ, gateN)):
                            cols = slice(q * P, (q + 1) * P)
                            pe.matmul(bank[4 * s + q][:, :], wc_hi[:, l, cols], agg_lo[s][:, :], start=False,
                                      stop=True).then_inc(ready, 1)

            pe.wait_ge(whD, 2)
            pe.wait_ge(wcD, LAYERS)
            transpose_start(0, 0)
            turns3(0, first=True)
            with pe.Fori(1, NG // 2 - 1) as i:
                turns3(i)
            turns3(NG // 2 - 1, last=True)
            for s in range(2):
                transpose_end(NG // 2 - 1, s, more=False)

        @block.vector
        def _(dve):
            dve.wait_ge(w_first, 16)
            nc.vector.tensor_copy(a1rep[:, :], wt("acol", 0, 1).broadcast_to([P, P])).then_inc(pre0, 1)
            nc.vector.tensor_copy(brep[:, :], wt("bcol").broadcast_to([P, P])).then_inc(pre0, 1)
            nc.vector.tensor_tensor(a12[:, :], wt("acol", 0, 1), wt("acol", 1, 2), ALU.add).then_inc(pre0, 1)
            dve.wait_ge(prod0, 1)
            nc.vector.tensor_copy(wa1[:, :], bank[4][:, 0:P]).then_inc(fold0, 1)
            nc.vector.tensor_copy(wplus[:, 0:P], wt("wwT"))
            nc.vector.tensor_copy(wplus[:, P:P + 1], bank[4][:, P:P + 1]).then_inc(fold0, 1)
            nc.vector.tensor_tensor(c0[:, :], bank[4][:, P + 1:P + 2], wt("ab"), ALU.add).then_inc(fold0, 1)

            def stats0(u):
                dve.wait_ge(in_x[u.p], 16 * (u.i + 1))
                n0.stats(nc, dve, u, lambda k: X[:, u.n * GROUP + k, :])

            def offset0(u):
                n0.offset(nc, dve, u)

            def copy_values(u):
                p = u.p
                dve.wait_ge(v0p, u.n + 1)
                if u.first(1):
                    dve.wait_ge(fold0, 3)
                if not u.first(2):
                    dve.wait_ge(exd0, u.n - 1)
                for b in range(2):
                    last = nc.vector.tensor_scalar(f0[p][:, 2 * b:2 * b + 2], halves(4)[b][:, :, P], c0[:, :], None,
                                                   ALU.add)
                last.then_inc(fd0, 1)
                if u.first(1):
                    dve.wait_ge(consts, 3)
                if not u.first(2):
                    dve.wait_ge(o0, u.n - 1)
                for b in range(2):
                    last = nc.vector.tensor_tensor(v0[p][:, 2 * b:2 * b + 2, 0:P], halves(4)[b][:, :, 0:P],
                                                   wt("brow").unsqueeze(1).broadcast_to([P, 2, P]), ALU.add)
                last.then_inc(v0d, 1)

            def update0(u):
                p = u.p
                dve.wait_ge(o0, u.n + 1)
                for b in range(2):
                    last = nc.vector.reciprocal(r0[p][:, 2 * b:2 * b + 2], halves(6)[b][:, :, P])
                last.then_inc(rd0, 1)
                dve.wait_ge(rd0, u.n + 1)
                for k in range(GROUP):
                    g = u.n * GROUP + k
                    last = nc.vector.scalar_tensor_tensor(X[:, g, :], halves(6)[k // 2][:, k % 2, 0:P], r0[p][:, k:k + 1],
                                                          X[:, g, :], ALU.mult, ALU.add)
                last.then_inc(x0, 1)

            skewed(dve, NG, [(2, stats0), (0, copy_values), (2, offset0), (-1, update0)])

            dve.wait_ge(x0, NG)

            def stats1(u):
                n1.stats(nc, dve, u, lambda k: X[:, u.n * PAIR + k, :])

            def offset1(u):
                n1.offset(nc, dve, u)

            def hide1(u):
                p = u.p
                dve.wait_ge(in1[p], 16 * (u.i + 1))
                if not u.first(2):
                    dve.wait_ge(score, CH * (u.n - 1))
                nc.vector.tensor_scalar(hide[p][:, :, :], adj1[p][:, :, :], 0.0, MASKED, ALU.is_equal,
                                        ALU.mult).then_inc(hideD, 1)

            def qk_lo(u):
                p = u.p
                dve.wait_ge(hi1, u.n + 1)
                nc.vector.scalar_tensor_tensor(q_lo[p][:, :, :].rearrange("p g n -> p (g n)"), bank[5][:, 0:PAIR * P], HD ** -0.5,
                                               q_hi[p][:, :, :].bitcast(F32).rearrange("p g n -> p (g n)"), ALU.mult, ALU.subtract)
                nc.vector.tensor_tensor(k_parts[p][:, 1, :, :].rearrange("p g n -> p (g n)"), bank[5][:, PAIR * P:2 * PAIR * P],
                                        k_parts[p][:, 0, :, :].bitcast(F32).rearrange("p g n -> p (g n)"),
                                        ALU.subtract).then_inc(lo1, 1)

            def shift(j):
                def stage(u):
                    p, g, c = u.p, j // 2, j % 2
                    dve.wait_ge(score, CH * u.n + j + 1)
                    if j == 0:
                        dve.wait_ge(edgeD, u.n + 1)
                    if not (u.first(1) and j < 2):
                        dve.wait_ge(probD, CH * u.n + j - 1)
                    dve.sem_inc(past_dve, 1)
                    for h in range(HC):
                        last = nc.vector.tensor_tensor_reduce(
                            out=neg[j % 2][:, h, :], in0=bank[j % 2][:, h * P:(h + 1) * P],
                            in1=edge[p][:, HC * c + h, g, :], scale=-1.0, scalar=-MASKED, op0=ALU.add,
                            op1=ALU.min, accum_out=nmax[j % 2][:, h:h + 1])
                    last.then_inc(shifted, 1)
                return stage

            def copy_probT(j):
                def stage(u):
                    dve.wait_ge(flip, CH * u.n + j + 1)
                    if not (u.first(1) and j < 2):
                        dve.wait_ge(pv, CH * u.n + j - 1)
                    nc.vector.tensor_copy(probT[j % 2][:, :, :].rearrange("p h n -> p (h n)"),
                                          bank[2 + j % 2][:, :]).then_inc(flipped, 1)
                return stage

            def normalize1(u):
                p = u.p
                of = bank[7][:, :].rearrange("p (h d) -> p h d", d=SLOT)
                dve.wait_ge(back1, u.n + 1)
                nc.vector.reciprocal(r1[:, :], of[:, :, HD]).then_inc(rd1, 1)
                dve.wait_ge(rd1, u.n + 1)
                if not u.first(2):
                    dve.wait_ge(tc1, u.n - 1)
                nc.vector.tensor_tensor(o1[p][:, :, :], of[:, :, 0:HD], r1[:, :].unsqueeze(2).broadcast_to([P, PAIR * H, HD]),
                                        ALU.mult).then_inc(o1d, 1)

            def update1(u):
                dve.wait_ge(wo1, u.n + 1)
                xs = X[:, bass.ds(u.n * PAIR, PAIR), :]
                nc.vector.tensor_tensor(xs, bank[7][:, 0:PAIR * P].rearrange("p (g n) -> p g n", g=PAIR), xs,
                                        ALU.add).then_inc(x1, 1)

            skewed(dve, NP, [(0, shift(1)), (0, copy_probT(0)), (1, qk_lo), (1, hide1), (0, shift(2)), (0, copy_probT(1)),
                             (-1, normalize1), (2, offset1), (0, shift(3)), (0, copy_probT(2)), (1, shift(0)),
                             (3, stats1), (-1, update1)])

            dve.wait_ge(x1, NP)
            nc.vector.tensor_reduce(fmax[:, :], wt("fw"), AXIS.X, ALU.max, negate=True).then_inc(soft2, 1)
            dve.wait_ge(soft2s, 1)
            nc.vector.reciprocal(frec[:, :], fsum[:, :]).then_inc(soft2, 1)
            dve.wait_ge(soft2, 2)
            nc.vector.tensor_scalar(fw[:, :], fexp[:, :], frec[:, :], None, ALU.mult)
            nc.vector.scalar_tensor_tensor(fwb[:, :], fexp[:, :], frec[:, :], wt("b2"), ALU.mult, ALU.mult).then_inc(soft2, 1)

            def degrees(u):
                p = u.p
                dve.wait_ge(in_a2[p], 16 * (u.i + 1))
                nc.vector.tensor_tensor(a2[p][:, :, :], a2[p][:, :, :], ident[:, :].unsqueeze(1).broadcast_to([P, T2, P]),
                                        ALU.add).then_inc(plus2, 1)
                dve.wait_ge(plus2, 3 * u.n + 1)
                nc.vector.tensor_reduce(deg[p][:, :], a2[p][:, :, :], AXIS.X, ALU.add).then_inc(plus2, 1)
                dve.wait_ge(plus2, 3 * u.n + 2)
                nc.vector.scalar_tensor_tensor(degs[p][:, :], deg[p][:, :], 0.0, deg[p][:, :], ALU.is_equal, ALU.add).then_inc(degD, 1)

            def scale_rows(u):
                p = u.p
                dve.wait_ge(degp, u.n + 1)
                if not u.first(2):
                    dve.wait_ge(normD, 2 * (u.n - 1))
                nc.vector.scalar_tensor_tensor(dinv[p][:, :], deg[p][:, :], 0.0, dpow[p][:, :], ALU.not_equal,
                                               ALU.mult).then_inc(plus2, 1)
                dve.wait_ge(plus2, 3 * u.n + 3)
                for t in range(T2):
                    last = nc.vector.tensor_scalar(a2[p][:, t, :], a2[p][:, t, :], dinv[p][:, t:t + 1], None, ALU.mult)
                last.then_inc(rows2, 1)

            def stats2(u):
                p = u.p
                dve.wait_ge(in_x2[p], 256 * (u.i + 1))
                n2.stats(nc, dve, u, lambda k: x2[p][:, k, :])

            def offset2(u):
                n2.offset(nc, dve, u)

            def copy_y(u):
                for l in range(2):
                    dve.wait_ge(y2, 2 * u.n + l + 1)
                    if not u.first(1):
                        dve.wait_ge(hid2, 4 * u.n)
                    nc.vector.tensor_copy(yT[:, l, :], bank[1 + l][:, :]).then_inc(y2d, 1)

            def copy_s2T(u):
                for l in range(2):
                    dve.wait_ge(s2p, 2 * u.n + l + 1)
                    if not u.first(1):
                        dve.wait_ge(t2, 2 * u.n)
                    used = NN if l == 0 else len(ROWS)
                    nc.vector.tensor_copy(rows_of(s2T[:, l, :])[:, :, 0:used], rows_of(bank[1 + l][:, :])[:, :, 0:used]).then_inc(s2d, 1)

            def copy_s2(u):
                for l in range(2):
                    dve.wait_ge(t2, 2 * u.n + l + 1)
                    if not u.first(1):
                        dve.wait_ge(o2, 2 * u.n)
                    nc.vector.tensor_copy(s2[:, TILES * l:TILES * (l + 1), :].rearrange("p t c -> p (t c)"),
                                          bank[3 + l][:, :]).then_inc(t2d, 1)

            def fuse(u):
                a, b = rows_of(g2[:, 0, :]), rows_of(g2[:, 1, :])
                f, fa = rows_of(f2[:, :]), rows_of(f2a[:, :])
                dve.wait_ge(o2d, 2 * u.n + 2)
                if not u.first(1):
                    dve.wait_ge(b2, u.n)
                nc.vector.tensor_tensor(fa[:, :, 0:15], a[:, :, 0:15], b[:, :, 0:15], ALU.add)
                nc.vector.tensor_copy(f[:, :, 15:NN], a[:, :, 15:NN]).then_inc(f2d, 1)
                dve.wait_ge(f2d, 3 * u.n + 1)
                nc.vector.tensor_tensor(f[:, :, 0:1], fa[:, :, 0:1], b[:, :, 15:16], ALU.add)
                nc.vector.tensor_copy(f[:, :, 1:3], fa[:, :, 1:3]).then_inc(f2d, 1)
                nc.vector.tensor_tensor(f[:, :, 3:15], fa[:, :, 3:15], b[:, :, 16:28], ALU.add).then_inc(f2d, 1)

            def update2(u):
                p = u.p
                dve.wait_ge(b2, u.n + 1)
                if not u.first(2):
                    dve.wait_ge(out2[p], 64 * u.i)
                nc.vector.tensor_tensor(xn2[p][:, :, :].rearrange("p t c -> p (t c)"), bank[7][:, :],
                                        x2[p][:, 0:TILES, :].rearrange("p t c -> p (t c)"), ALU.add).then_inc(x2d, 1)

            skewed(dve, NB, [(1, degrees), (1, stats2), (1, scale_rows), (1, offset2), (0, copy_y), (0, copy_s2T), (0, copy_s2),
                             (0, fuse), (0, update2)])

            for p in range(2):
                dve.wait_ge(out2[p], 64 * NB // 2)
            nc.vector.tensor_copy(wh_hi[:, :], wt("whhT")).then_inc(whD, 1)
            nc.vector.tensor_tensor(brz[:, :], wt("bih"), wt("bhh"), ALU.add)
            dve.wait_ge(whD, 1)
            nc.vector.tensor_tensor(wh_lo[:, :], wt("whhT"), wh_hi[:, :].bitcast(F32), ALU.subtract).then_inc(whD, 1)
            for l in range(LAYERS):
                dve.wait_ge(wcH, l + 1)
                nc.vector.tensor_tensor(wc_lo[:, l, :], bank[l][:, 0:GATES * P], wc_hi[:, l, :].bitcast(F32),
                                        ALU.subtract).then_inc(wcD, 1)

            def stats3(i, s):
                u = Unit(i, s)
                n3.stats(nc, dve, u, lambda k: X[:, u.n * GROUP + k, :])

            def offset3(i, s):
                n3.offset(nc, dve, Unit(i, s))

            def edges3(i, s):
                dve.wait_ge(in3[s], 16 * (i + 1))
                if not (isinstance(i, int) and i == 0):
                    dve.wait_ge(aggP, nth(LAYERS * i, s))
                nc.vector.tensor_scalar(edge3[s][:, :], adj3[s][:, :], 0.0, None, ALU.not_equal).then_inc(edge3d[s], 1)

            def start_rest(i, s):
                dve.wait_ge(startS[s], i + 1)
                if not (isinstance(i, int) and i == 0):
                    dve.wait_ge(keptD, nth(LAYERS * (i - 1) + 1, s))
                nc.vector.tensor_copy(start_T[s][:, :], bank[4 * s + 3][:, :])
                nc.vector.tensor_tensor(h_lo[s][:, :], bank[4 * s + 3][:, :], h_hi[s][:, :].bitcast(F32),
                                        ALU.subtract).then_inc(split3[s], 1)

            def agg_lower(i, l, s):
                dve.wait_ge(aggH, nth(LAYERS * i + l + 1, s))
                nc.vector.tensor_tensor(agg_lo[s][:, :], bank[4 * s + 2][:, :], agg_hi[s][:, :].bitcast(F32),
                                        ALU.subtract).then_inc(aggL, 1)

            def pre_candidate(i, l, s):
                c = LAYERS * i + l
                dve.wait_ge(resetD, nth(c + 1, s))
                dve.wait_ge(gateN, nth(c + 1, s))
                nc.vector.scalar_tensor_tensor(mixed[s][:, :], bank[4 * s + 3][:, :], wt("bhh", 2, 3), reset[s][:, :],
                                               ALU.add, ALU.mult).then_inc(dotD, 1)
                dve.wait_ge(dotD, nth(c + 1, s))
                nc.vector.tensor_tensor(cand[s][:, :], bank[4 * s + 2][:, :], mixed[s][:, :], ALU.add).then_inc(preD, 1)

            def mix(i, l, s):
                c = LAYERS * i + l
                dve.wait_ge(candD, nth(c + 1, s))
                dve.wait_ge(keepD, nth(c + 1, s))
                nc.vector.tensor_tensor(mixed[s][:, :], keep_[s][:, :], cand[s][:, :], ALU.mult).then_inc(mixD, 1)

            def new_state(i, l, s):
                c = LAYERS * i + l
                dve.wait_ge(mixD, nth(c + 1, s))
                dve.wait_ge(keptD, nth(c + 1, s))
                nc.vector.tensor_tensor(state_T[s][:, :], mixed[s][:, :], kept[s][:, :], ALU.add).then_inc(stateD, 1)
                if l < LAYERS - 1:
                    dve.wait_ge(stateD, nth(c + 1, s))
                    nc.vector.tensor_copy(h_hi[s][:, :], state_T[s][:, :]).then_inc(hiD, 1)
                    dve.wait_ge(hiD, nth((LAYERS - 1) * i + l + 1, s))
                    nc.vector.tensor_tensor(h_lo[s][:, :], state_T[s][:, :], h_hi[s][:, :].bitcast(F32),
                                            ALU.subtract).then_inc(split3[s], 1)

            def update3(i, s):
                dve.wait_ge(flipE[s], i + 1)
                for k in range(GROUP):
                    g = (2 * i + s) * GROUP + k
                    at = (2 * i + s) * GROUP + k
                    last = nc.vector.scalar_tensor_tensor(X[:, g, :], bank[4 * s + 3][:, k * P:(k + 1) * P],
                                                          weights[:, bass.ds(COL["nmask"][0] + at, 1)], X[:, g, :], ALU.mult, ALU.add)
                last.then_inc(x3[s], 1)

            def turns3(i, first=False, last=False):
                for l in range(LAYERS):
                    for s in range(2):
                        post = (i, l, 0) if s else (i, l - 1, 1) if l else (i - 1, LAYERS - 1, 1)
                        busy = not (first and l == s == 0)
                        if busy:
                            pre_candidate(*post)
                        if l == 0 and not first:
                            update3(i - 1, s)
                        if busy:
                            mix(*post)
                        agg_lower(i, l, s)
                        if busy:
                            new_state(*post)
                        if l == 0 and s == 0:
                            start_rest(i, 1)
                            edges3(i, 1)
                        if l == 4 and s == 1 and not last:
                            start_rest(i + 1, 0)
                            edges3(i + 1, 0)
                        if l == 1 and not last:
                            stats3(i + 1, s)
                        if l == 2 and not last:
                            offset3(i + 1, s)

            for s in range(2):
                stats3(0, s)
            for s in range(2):
                offset3(0, s)
            start_rest(0, 0)
            edges3(0, 0)
            turns3(0, first=True)
            with dve.Fori(1, NG // 2 - 1) as i:
                turns3(i)
            turns3(NG // 2 - 1, last=True)
            post = (NG // 2 - 1, LAYERS - 1, 1)
            pre_candidate(*post)
            mix(*post)
            new_state(*post)
            for s in range(2):
                update3(NG // 2 - 1, s)


def kernel(**inputs):
    import concourse.bacc as _bacc
    from concourse.bass_utils import run_bass_kernel_spmd as _run

    a = {k: np.asarray(v) for k, v in inputs.items()}
    x, adj = a["x"], a["adj"]

    def rows(v):
        return np.broadcast_to(v.reshape(1, -1), (P, v.size))

    W1, W2 = a["L2_gnn_W1"], a["L2_gnn_W2"]
    part = {
        "ww": a["L0_gnn_W_w"], "wwT": a["L0_gnn_W_w"].T, "bcol": a["L0_gnn_W_b"][:, None],
        "acol": a["L0_gnn_a_w"].reshape(2, P).T, "ab": rows(a["L0_gnn_a_b"]), "brow": rows(a["L0_gnn_W_b"]),
        "wqT": a["L1_gnn_W_q"].T, "wkT": a["L1_gnn_W_k"].T, "wvT": a["L1_gnn_W_v"].T, "woT": a["L1_gnn_W_o"].T,
        "we": rows(a["L1_gnn_W_e"]),
        "w1": W1.transpose(1, 0, 2).reshape(P, -1), "b1": a["L2_gnn_b1"].reshape(10, P).T,
        "w2": W2.reshape(10, P, P).transpose(1, 0, 2).reshape(P, -1), "b2": a["L2_gnn_b2"].T,
        "fw": rows(a["L2_gnn_fusion_w"]),
        "gwT": a["L3_gnn_weight"].transpose(2, 0, 1).reshape(P, -1),
        "wihT": a["L3_gnn_w_ih"].T, "whhT": a["L3_gnn_w_hh"].T,
        "bih": a["L3_gnn_b_ih"].reshape(GATES, P).T, "bhh": a["L3_gnn_b_hh"].reshape(GATES, P).T,
        "nmask": a["nodemask"].T,
    }
    arrays = {
        "x": x.transpose(1, 0, 2), "adj": adj.transpose(1, 0, 2), "adjT": adj.transpose(2, 0, 1),
        "weights": np.concatenate([part[n] for n, _ in _SIZES], axis=1), "blocks": pack_blocks(adj),
    }
    arrays = {k: np.ascontiguousarray(v) for k, v in arrays.items()}
    nc = _bacc.Bacc("TRN2", target_bir_lowering=False, num_devices=1)
    ins = {k: nc.dram_tensor(f"in_{k}", v.shape, mybir.dt.from_np(v.dtype), kind="ExternalInput").ap()
           for k, v in arrays.items()}
    out = nc.dram_tensor("out", (P, B, P), F32, kind="ExternalOutput").ap()
    build(nc, ins, out)
    r = _run(nc, [{f"in_{k}": v for k, v in arrays.items()}], core_ids=[0])
    return np.ascontiguousarray(r.results[0]["out"].transpose(1, 0, 2))


def pack_blocks(adj):
    packed = np.zeros((P, NB, 2, TILES, P), adj.dtype)
    for b in range(B):
        batch, tile, s = b // BG, b % BG // 4, b % 4 * SLOT
        packed[s:s + NN, batch, 0, tile, s:s + NN] = adj[b, :NN, :NN]
        for r, (n, g) in enumerate(ROWS):
            for c, (m, k) in enumerate(ROWS):
                if g == k:
                    packed[s + r, batch, 1, tile, s + c] = adj[b, n, m]
    return packed
```

```python
from contextlib import ExitStack

import numpy as np

import concourse.bass as bass
from concourse import mybir

F32 = mybir.dt.float32
F32R = mybir.dt.float32r
BF16 = mybir.dt.bfloat16
ALU = mybir.AluOpType
ACT = mybir.ActivationFunctionType
AXIS = mybir.AxisListType

B = 64
P = 128
EPS = 1e-5
GROUP = 4
NG = B // GROUP
W = GROUP * P
MASKED = -1e30

H = 8
HD = P // H
PAIR = 2
NP = B // PAIR
HC = 4
CH = PAIR * H // HC

NN = 25
HID = 256
SLOT = 32
RUNS = [(0, 0, 15), (15, 0, 15)]
ROWS = [(n, n, 1) for n in range(9)] + [(n, n, 2) for n in range(9, 15)] + [(15, 0, 2)] + \
       [(15 + n, n, 4) for n in (3, 4, 5, 9, 10, 11)] + [(15 + n, n, 3) for n in (6, 7, 8, 12, 13, 14)]
SPANS = {1: [(0, 9)], 2: [(9, 16)], 3: [(21, 24), (27, 30)], 4: [(18, 21), (24, 27)]}
TILES = 4
BG = 4 * TILES
NB = B // BG
T2 = 2 * TILES

LAYERS = 5
GATES = 3

_SIZES = [("ww", P), ("wwT", P), ("bcol", 1), ("acol", 2), ("ab", 1), ("brow", P),
          ("wqT", P), ("wkT", P), ("wvT", P), ("woT", P), ("we", H),
          ("w1", 5 * HID), ("b1", 10), ("w2", 10 * P), ("b2", 5), ("fw", 5),
          ("gwT", LAYERS * P), ("wihT", GATES * P), ("whhT", GATES * P), ("bih", GATES), ("bhh", GATES), ("nmask", B)]
COL, _at = {}, 0
for _n, _s in _SIZES:
    COL[_n] = (_at, _at + _s)
    _at += _s
NCOL = _at
FIRST = COL["wqT"][0]


class Unit:

    def __init__(self, i, p, U=2):
        self.i, self.p, self.U = i, p, U

    @property
    def n(self):
        return self.U * self.i + self.p

    def back(self, k):
        q = self.p - k
        return Unit(self.i + q // self.U, q % self.U, self.U)

    def first(self, k):
        return isinstance(self.i, int) and self.n < k


def skewed(eng, count, stages, U=2, margin=2):
    lo, hi = min(s for s, _ in stages), max(s for s, _ in stages)
    begin = -(-(margin - lo) // U) * U
    end = (count - hi) // U * U

    def turn(i, p):
        for shift, stage in stages:
            q = p + shift
            u = Unit(i + q // U, q % U, U)
            if not isinstance(i, int) or 0 <= u.n < count:
                stage(u)

    if end - begin < 2 * U:
        begin = end = count - lo
    for t in range(-hi, begin):
        turn(t // U, t % U)
    if begin < end:
        with eng.Fori(begin // U, end // U) as i:
            for p in range(U):
                turn(i, p)
        for t in range(end, count - lo):
            turn(t // U, t % U)


class Norm:

    def __init__(self, sb, sem, name, K, mhalf, ready):
        self.K, self.mhalf, self.ready = K, mhalf, ready
        self.st = [sb(f"{name}_st{p}", [P, K, 6], F32) for p in range(2)]
        self.mv = [sb(f"{name}_mv{p}", [P, K, 2], F32) for p in range(2)]
        self.ve = [sb(f"{name}_ve{p}", [P, K], F32) for p in range(2)]
        self.rstd = [sb(f"{name}_rstd{p}", [P, K], F32) for p in range(2)]
        self.shift = [sb(f"{name}_shift{p}", [P, K], F32) for p in range(2)]
        self.bn, self.ag, self.vd = sem(f"{name}_bn"), sem(f"{name}_ag"), sem(f"{name}_var")
        self.pw, self.sh, self.done = sem(f"{name}_pow"), sem(f"{name}_shift"), sem(f"{name}_done")

    def tile_stats(self, nc, u, x, tiles):
        for k in tiles:
            last = nc.vector.bn_stats(self.st[u.p % 2][:, k, :], x(k))
        if tiles[-1] == self.K - 1:
            last.then_inc(self.bn, 1)

    def unit_stats(self, nc, dve, u):
        p = u.p % 2
        dve.wait_ge(self.bn, u.n + 1)
        if not u.first(2):
            dve.wait_ge(self.done, u.n - 1)
        dve.sem_inc(self.ready, 1)
        for k in range(self.K):
            last = nc.vector.bn_aggr(self.mv[p][:, k, :], self.st[p][:, k, :])
        last.then_inc(self.ag, 1)
        dve.wait_ge(self.ag, u.n + 1)
        nc.vector.tensor_scalar(self.ve[p][:, :], self.mv[p][:, :, 1], EPS, None, ALU.add).then_inc(self.vd, 1)

    def stats(self, nc, dve, u, x):
        self.tile_stats(nc, u, x, range(self.K))
        self.unit_stats(nc, dve, u)

    def power(self, nc, pool, u):
        p = u.p % 2
        pool.wait_ge(self.vd, u.n + 1)
        if not u.first(2):
            pool.wait_ge(self.done, u.n - 1)
        nc.gpsimd.tensor_tensor(self.rstd[p][:, :], self.ve[p][:, :], self.mhalf[:, 0:self.K],
                                ALU.pow).then_inc(self.pw, 1)

    def offset(self, nc, dve, u):
        p = u.p % 2
        dve.wait_ge(self.pw, u.n + 1)
        nc.vector.scalar_tensor_tensor(self.shift[p][:, :], self.mv[p][:, :, 0], -1.0, self.rstd[p][:, :],
                                       ALU.mult, ALU.mult).then_inc(self.sh, 1)

    def apply(self, nc, act, u, x, out):
        p = u.p % 2
        act.wait_ge(self.sh, u.n + 1)
        for k in range(self.K):
            last = nc.scalar.activation(out(k), x(k), ACT.Relu, bias=self.shift[p][:, k:k + 1],
                                        scale=self.rstd[p][:, k:k + 1])
        last.then_inc(self.done, 1)


def build(nc, ins, out):
    x_in, adj_in, adjT_in, blocks_in, w_in = (ins[k] for k in ("x", "adj", "adjT", "blocks", "weights"))
    ctx = ExitStack()
    with ctx:
        def sem(name):
            return ctx.enter_context(nc.semaphore(name))

        def keep(name, shape, dt):
            return ctx.enter_context(nc.sbuf_tensor(name, shape, dt))

        bank = [ctx.enter_context(nc.psum_tensor(f"bank{i}", [P, W], F32)) for i in range(8)]

        X = keep("X", [P, B, P], F32)
        weights = keep("weights", [P, NCOL], F32)
        ident = keep("ident", [P, P], F32)
        ident_bf = keep("ident_bf", [P, P], BF16)
        mhalf = keep("mhalf", [P, 8], F32)

        def wt(name, a=0, b=None):
            lo, hi = COL[name]
            return weights[:, lo + a:(hi if b is None else lo + b)]

        consts = sem("consts")
        past_dve, past_pool, past_sp = sem("past_dve"), sem("past_pool"), sem("past_sp")

        def region():
            stack = ExitStack()
            return stack, lambda name, shape, dt: stack.enter_context(nc.sbuf_tensor(name, shape, dt))

        def both(sb, name, dt=F32, shape=(P, W)):
            return [sb(f"{name}_{s}", list(shape), dt) for s in range(2)]

        over2, sb = region()
        state_T, state_n = both(sb, "state_T"), both(sb, "state_n")
        reset, update = both(sb, "reset"), both(sb, "update")
        h_hi, h_lo, agg_hi, agg_lo = (both(sb, n, F32R) for n in ("h_hi", "h_lo", "agg_hi", "agg_lo"))
        kept, cand, mixed = both(sb, "kept"), both(sb, "cand"), both(sb, "mixed")
        over2.close()

        packed2, sb = region()
        x2 = sb("x2", [P, 2, NB * TILES, P], F32)
        a2 = sb("a2", [P, NB, T2, P], F32)
        n2 = Norm(sb, sem, "n2", T2, mhalf, past_dve)
        deg, degs, dpow, dinv = (sb(n, [P, NB, T2], F32) for n in ("deg", "degs", "dpow", "dinv"))

        layer0, sb = region()
        adjT0 = [sb(f"adjT0_{p}", [P, GROUP, P], F32) for p in range(2)]
        ex0 = [sb(f"ex0_{p}", [P, GROUP, P], F32) for p in range(2)]
        u0 = [sb(f"u0_{p}", [P, GROUP, P], F32) for p in range(2)]
        layer0.close()

        layer1, sb = region()
        probT = [sb(f"probT_{p}", [P, HC, P], F32) for p in range(2)]
        oT1 = [sb(f"oT1_{p}", [P, CH, P], F32) for p in range(2)]
        o1 = [sb(f"o1_{p}", [P, PAIR * H, HD], F32) for p in range(2)]
        oc1 = [sb(f"oc1_{p}", [P, PAIR, P], F32) for p in range(2)]

        n0 = Norm(sb, sem, "n0", GROUP, mhalf, past_dve)
        h0n = [sb(f"h0n_{p}", [P, GROUP, P], F32) for p in range(2)]
        h0T = [sb(f"h0T_{p}", [P, GROUP, P], F32) for p in range(2)]
        a1rep = sb("a1rep", [P, P], F32)
        brep = sb("brep", [P, P], F32)
        a12 = sb("a12", [P, 1], F32)
        wa1 = sb("wa1", [P, P], F32)
        wplus = sb("wplus", [P, P + 1], F32)
        c0 = sb("c0", [P, 1], F32)
        v0 = [sb(f"v0_{p}", [P, GROUP, P + 1], F32) for p in range(2)]
        f0 = [sb(f"f0_{p}", [P, GROUP], F32) for p in range(2)]
        r0 = [sb(f"r0_{p}", [P, GROUP], F32) for p in range(2)]

        n1 = Norm(sb, sem, "n1", PAIR, mhalf, past_dve)
        adj1 = [sb(f"adj1_{p}", [P, PAIR, P], F32) for p in range(2)]
        h1n = [sb(f"h1n_{p}", [P, PAIR, P], F32) for p in range(2)]
        h1T = [sb(f"h1T_{p}", [P, PAIR, P], F32) for p in range(2)]
        q_hi = [sb(f"q_hi_{p}", [P, PAIR, P], F32R) for p in range(2)]
        q_lo = [sb(f"q_lo_{p}", [P, PAIR, P], F32R) for p in range(2)]
        k_parts = [sb(f"k_parts_{p}", [P, 2, PAIR, P], F32R) for p in range(2)]
        k_diag = [sb(f"k_diag_{p}", [P, 2, PAIR, H, P], F32R) for p in range(2)]
        v1 = [sb(f"v1_{p}", [P, PAIR, H, SLOT], F32) for p in range(2)]
        edge = [sb(f"edge_{p}", [P, H, PAIR, P], F32) for p in range(2)]
        hide = [sb(f"hide_{p}", [P, PAIR, P], BF16) for p in range(2)]
        neg = [sb(f"neg_{p}", [P, HC, P], F32) for p in range(2)]
        nmax = [sb(f"nmax_{p}", [P, HC], F32) for p in range(2)]
        prob = [sb(f"prob_{p}", [P, HC, P], F32) for p in range(2)]
        r1 = sb("r1", [P, PAIR * H], F32)
        layer1.close()

        layer2, sb = region()
        normT = sb("normT", [P, NB, T2, P], F32)
        h2 = [sb(f"h2_{p}", [P, T2, P], F32) for p in range(2)]
        yT = sb("yT", [P, 2, W], F32)
        hidT = sb("hidT", [P, 2, 2, W], F32)
        s2T = sb("s2T", [P, 2, W], F32)
        s2 = sb("s2", [P, T2, P], F32)
        g2 = sb("g2", [P, 2, W], F32)
        f2 = sb("f2", [P, W], F32)
        f2a = sb("f2a", [P, W], F32)
        xn2 = [sb(f"xn2_{p}", [P, TILES, P], F32) for p in range(2)]
        fmax, fexp, fsum, frec, fw, fwb = (sb(n, [P, k], F32) for n, k in (
            ("fmax", 1), ("fexp", 5), ("fsum", 1), ("frec", 1), ("fw", 5), ("fwb", 5)))

        n3 = Norm(sb, sem, "n3", GROUP, mhalf, past_dve)
        adj3, edge3 = both(sb, "adj3"), both(sb, "edge3")
        start_n, start_T = both(sb, "start_n"), both(sb, "start_T")
        wc_hi, wc_lo = (sb(n, [P, LAYERS, GATES * P], F32R) for n in ("wc_hi", "wc_lo"))
        wh_hi, wh_lo = (sb(n, [P, GATES * P], F32R) for n in ("wh_hi", "wh_lo"))
        brz = sb("brz", [P, GATES], F32)
        layer2.close()
        packed2.close()

        def two(name):
            return [sem(f"{name}_{s}") for s in range(2)]

        in3, edge3d, flip0, flip3, natural3, flipE, split3 = (two(n) for n in (
            "in3", "edge3_done", "start_transposed", "state_transposed", "state_n_done", "end_transposed", "split_done"))
        startS, x3 = two("start_hi_done"), two("x3_done")
        aggP, aggH, aggL, gateR, gateZ, gateN, resetD, updateD, dotD, preD, candD, keptD, mixD, stateD, hiD = (
            sem(n) for n in ("agg_product", "agg_hi_done", "agg_lo_done", "reset_ready", "update_ready", "cand_ready",
                             "reset_done", "update_done", "reset_dot_done", "pre_done", "cand_done",
                             "kept_done", "mix_done", "state_done", "h_hi_done"))

        def nth(count, s):
            return 2 * count + s - 1

        def half_of(count, s, half):
            return 2 * nth(count, s) + half - 1

        HALVES = [slice(h * W // 2, (h + 1) * W // 2) for h in range(2)]

        wcP, wcH, wcD, whD = (sem(n) for n in ("wc_product", "wc_hi_done", "wc_done", "wh_done"))

        in_x2, in_a2 = sem("in_x2"), sem("in_a2")
        clear2, clear3, soft2, soft2s, plus2, degD, degp, dinvD, rows2, flip2 = (sem(s) for s in (
            "clear2", "clear3", "soft2", "soft2_exp", "plus2", "deg_done", "deg_power", "dinv_done", "rows2", "flip2"))
        normD = [sem(f"normT_done_{l}") for l in range(2)]
        y2, y2d, hid2, hid2d, s2p, s2d, t2, t2d, o2, o2d, f2d, b2, x2d = (sem(s) for s in (
            "y2", "y2_done", "hid2", "hid2_done", "s2T_product", "s2T_done", "s2_transposed", "s2_done", "o2",
            "g2_done", "f2_done", "back2", "xn2_done"))
        out2 = [sem(f"x2_written_{p}") for p in range(2)]

        w_first, w_rest = sem("w_first"), sem("w_rest")
        in1 = [sem(f"in1_{p}") for p in range(2)]
        in_k = [sem(f"in_k_{p}") for p in range(2)]
        clear1, hideD, edgeD = sem("clear1"), sem("hide_done"), sem("edge_done")
        t1, hT1, qk1, hi1, lo1, vp1, vd1 = (sem(s) for s in (
            "t1_done", "hT1_done", "qk1_product", "hi1_done", "lo1_done", "v1_product", "v1_done"))
        score, shifted, probD, flip, flipped, pv, flippedS = (sem(s) for s in (
            "scores_ready", "shifted_ready", "probs_ready", "probs_transposed", "probT_ready", "pv_done", "last_probT_ready"))
        oT1d, back1, rd1, o1d, tc1, oc1d, wo1, x1 = (sem(s) for s in (
            "oT1_done", "back1_done", "r1_done", "o1_done", "oc1_product", "oc1_done", "wo1_done", "x1_done"))
        in_x = [sem(f"in_x_{p}") for p in range(2)]
        in_adjT = [sem(f"in_adjT_{p}") for p in range(2)]
        pre0, prod0, fold0 = sem("pre0"), sem("prod0"), sem("fold0")
        t0, hT0, e0, v0p, v0d, fd0, exd0, ud0, o0, rd0, x0 = (sem(s) for s in (
            "t0_done", "hT0_done", "e0_done", "v0_product", "v0_done", "f0_done", "exp0_done", "u0_done",
            "o0_done", "r0_done", "x0_done"))
        x_out = sem("x_out")

        def halves(lo):
            return [bank[lo + b][:, 0:2 * (P + 1)].rearrange("p (g c) -> p g c", g=2) for b in range(2)]

        def tile2(b, k):
            return x2[:, k // TILES, TILES * b + k % TILES, :]

        GATHERS = 16 * 4 * (1 + len(RUNS))
        FIRST_BATCH = FIRST_PAIR = Unit(0, 0)
        SECOND_PAIR = Unit(0, 1)

        def when(n, step, *args):
            return lambda u: step(*args) if isinstance(u.i, int) and u.n == n else None

        def without(n, stage):
            return lambda u: None if u.first(n) else stage(u)

        def folds(step):
            return (1, lambda u: step(u.n)), (0, lambda u: step(LAYERS - 1) if u.n == NB - 1 else None)

        def rows_of(a):
            return a.rearrange("p (g s) -> p g s", s=SLOT)

        def slots(a, g):
            if g == 0:
                return rows_of(a)[:, :, 0:NN]
            if len(SPANS[g]) == 1:
                return rows_of(a)[:, :, slice(*SPANS[g][0])]
            lo = SPANS[g][0][0]
            return rows_of(a)[:, :, 18:30].rearrange("p g (s k) -> p g s k", k=3)[:, :, (lo - 18) // 3::2, :]

        block = ctx.enter_context(nc.Block())

        @block.sync
        def _(sp):
            sp.dma_start(weights[:, 0:FIRST], w_in[:, 0:FIRST]).then_inc(w_first, 16)

            def load_x(u):
                if not u.first(2):
                    sp.wait_ge(n0.bn, u.n - 1)
                sp.sem_inc(past_sp, 1)
                sp.dma_start(X[:, bass.ds(u.n * GROUP, GROUP), :],
                             x_in[:, bass.ds(u.n * GROUP, GROUP), :]).then_inc(in_x[u.p], 16)

            def load_adjT(u):
                if not u.first(2):
                    sp.wait_ge(ud0, u.n - 1)
                sp.sem_inc(past_sp, 1)
                sp.dma_start(adjT0[u.p][:, :, :],
                             adjT_in[:, bass.ds(u.n * GROUP, GROUP), :]).then_inc(in_adjT[u.p], 16)
                if u.first(1):
                    sp.dma_start(weights[:, FIRST:NCOL], w_in[:, FIRST:NCOL]).then_inc(w_rest, 16)

            skewed(sp, NG, [(3, load_x), (0, load_adjT)])
            sp.dma_start(a2[:, :, :, :].rearrange("p b t c -> p (b t c)"), blocks_in[:, :]).then_inc(in_a2, 16)

            def load_adj1(u):
                if not u.first(2):
                    sp.wait_ge(edgeD, u.n - 1)
                    sp.wait_ge(hideD, u.n - 1)
                sp.sem_inc(past_sp, 1)
                sp.dma_start(adj1[u.p % 2][:, :, :], adj_in[:, bass.ds(u.n * PAIR, PAIR), :]).then_inc(in1[u.p % 2], 16)

            def spread_k(u):
                p = u.p % 2
                sp.wait_ge(lo1, u.n + 1)
                sp.sem_inc(past_sp, 1)
                if u.first(1):
                    sp.wait_ge(clear1, 3)
                if not u.first(2):
                    sp.wait_ge(score, CH * (u.n - 1))
                sp.sem_inc(past_sp, 1)
                for h in range(H):
                    rows = slice(HD * h, HD * (h + 1))
                    sp.dma_start(k_diag[p][rows, :, :, h, :].bitcast(F32), k_parts[p][rows, :, :, :].bitcast(F32)).then_inc(in_k[p], 16)

            def gather_slot(b, s):
                tiles = bass.ds(TILES * b, TILES)
                graphs = bass.ds(BG * b + s, TILES, 4)
                sp.dma_start(x2[SLOT * s:SLOT * s + NN, 0, tiles, :], X[0:NN, graphs, :]).then_inc(in_x2, 16)
                for row, node, count in RUNS:
                    sp.dma_start(x2[SLOT * s + row:SLOT * s + row + count, 1, tiles, :],
                                 X[node:node + count, graphs, :]).then_inc(in_x2, 16)

            def gather2(u):
                if u.p == U1 - 1:
                    sp.wait_ge(x1, u.n + 1)
                    sp.sem_inc(past_sp, 1)
                    if u.first(U1):
                        sp.wait_ge(clear2, 1)
                    else:
                        sp.wait_ge(in_x2, GATHERS * u.i)
                    sp.sem_inc(past_sp, 1)
                    gather_slot(u.i, 0)
                elif u.p < 3 and not u.first(U1):
                    gather_slot(u.i - 1, u.p + 1)

            U1 = BG // PAIR
            skewed(sp, NP, [(2, load_adj1), (2, spread_k), (-2, gather2)], U=U1)
            for s in range(1, 4):
                gather_slot(NB - 1, s)

            def load3(i, s):
                if isinstance(i, int) and i == 0:
                    pass
                else:
                    sp.wait_ge(edge3d[s], i)
                    sp.sem_inc(past_sp, 1)
                sp.dma_start(adj3[s][:, :], adj_in[:, bass.ds((2 * i + s) * GROUP, GROUP), :].rearrange("p g n -> p (g n)")
                             ).then_inc(in3[s], 16)

            for s in range(2):
                load3(0, s)
            for b in range(NB):
                p = b % 2
                sp.wait_ge(x2d, b + 1)
                for s in range(4):
                    rows = slice(SLOT * s, SLOT * s + NN)
                    sp.dma_start(X[0:NN, slice(BG * b + s, BG * (b + 1), 4), :], xn2[p][rows, :, :]).then_inc(out2[p], 16)

            def store3(i, s):
                sp.wait_ge(x3[s], i + 1)
                sp.sem_inc(past_sp, 1)
                rows = bass.ds((2 * i + s) * GROUP, GROUP)
                sp.dma_start(out[:, rows, :], X[:, rows, :]).then_inc(x_out, 16)

            with sp.Fori(1, NG // 2) as i:
                for s in range(2):
                    load3(i, s)
                for s in range(2):
                    store3(i - 1, s)
            for s in range(2):
                store3(NG // 2 - 1, s)
            sp.wait_ge(x_out, 16 * NG)

        @block.gpsimd
        def _(pool):
            nc.gpsimd.memset(mhalf[:, :], -0.5)
            nc.gpsimd.memset(ident[:, :], 1.0).then_inc(consts, 1)
            pool.wait_ge(consts, 1)
            nc.gpsimd.affine_select(out=ident[:, :], in_=ident[:, :], compare_op=ALU.is_equal, fill=0.0, base=0,
                                    pattern=[[-1, P]], channel_multiplier=1).then_inc(consts, 1)
            pool.wait_ge(consts, 2)
            nc.gpsimd.tensor_copy(ident_bf[:, :], ident[:, :])
            for p in range(2):
                last = nc.gpsimd.memset(v0[p][:, :, P:P + 1], 1.0)
            last.then_inc(consts, 1)

            def u_product(u):
                p = u.p
                pool.wait_ge(exd0, u.n + 1)
                pool.wait_ge(in_adjT[p], 16 * (u.i + 1))
                if not u.first(2):
                    pool.wait_ge(o0, u.n - 1)
                nc.gpsimd.tensor_tensor(u0[p][:, :, :], ex0[p][:, :, :], adjT0[p][:, :, :], ALU.mult).then_inc(ud0, 1)

            def power0(u):
                n0.power(nc, pool, u)

            def clear_k(p):
                nc.gpsimd.memset(k_diag[p][:, :, :, :, :].bitcast(F32), 0.0).then_inc(clear1, 1)

            def clear_v():
                for p in range(2):
                    nc.gpsimd.memset(v1[p][:, :, :, HD + 1:SLOT], 0.0)
                    last = nc.gpsimd.memset(v1[p][:, :, :, HD:HD + 1], 1.0)
                last.then_inc(clear1, 1)

            def clear_x2():
                nc.gpsimd.memset(x2[:, :, :, :], 0.0).then_inc(clear2, 1)

            def power1(u):
                n1.power(nc, pool, u)

            skewed(pool, NG, [(3, power0), (0, u_product), (1, when(0, clear_k, 0)), (0, when(NG - 1, power1, FIRST_PAIR))])
            power1(SECOND_PAIR)
            clear_k(1)
            clear_v()

            def edges(u):
                p = u.p
                if u.first(1):
                    pool.wait_ge(w_rest, 16)
                if not u.first(2):
                    pool.wait_ge(shifted, CH * (u.n - 1))
                pool.wait_ge(in1[p], 16 * (u.i + 1))
                pool.sem_inc(past_pool, 1)
                for h in range(H):
                    last = nc.gpsimd.tensor_scalar(edge[p][:, h, :, :], adj1[p][:, :, :], wt("we", h, h + 1), 0.0,
                                                   ALU.mult, ALU.add)
                last.then_inc(edgeD, 1)

            def power_deg(u):
                if isinstance(u.i, int) and u.n < NB:
                    pool.wait_ge(degD, u.n + 1)
                    nc.gpsimd.tensor_tensor(dpow[:, u.n, :], degs[:, u.n, :], mhalf[:, 0:T2], ALU.pow).then_inc(degp, 1)

            def power2(u):
                n2.power(nc, pool, u)

            skewed(pool, NP, [(3, power_deg), (1, edges), (4, without(2, power1)), (0, when(NP - 1, power2, FIRST_BATCH)),
                             (0, when(0, clear_x2))])

            pool.wait_ge(x1, NP)
            nc.gpsimd.memset(s2T[:, :, :], 0.0)
            nc.gpsimd.memset(f2[:, :], 0.0).then_inc(clear3, 1)

            def power3(i, s):
                n3.power(nc, pool, Unit(i, s))

            skewed(pool, NB, [(3, without(1, power2))])
            for s in range(2):
                power3(0, s)

            def keep3(i, l, s):
                c = LAYERS * i + l
                pool.wait_ge(updateD, nth(c + 1, s))
                nc.gpsimd.tensor_tensor(kept[s][:, :], update[s][:, :], (start_T if l == 0 else state_T)[s][:, :],
                                        ALU.mult).then_inc(keptD, 1)

            def turns3(i, last=False):
                for l in range(LAYERS):
                    for s in range(2):
                        keep3(i, l, s)
                        if l == 3 and not last:
                            power3(i + 1, s)

            turns3(0)
            with pool.Fori(1, NG // 2 - 1) as i:
                turns3(i)
            turns3(NG // 2 - 1, last=True)

        @block.scalar
        def _(act):
            def apply0(u):
                p = u.p
                if not u.first(2):
                    act.wait_ge(t0, u.n - 1)
                n0.apply(nc, act, u, lambda k: X[:, u.n * GROUP + k, :], lambda k: h0n[p][:, k, :])

            def evac_hT(u):
                p = u.p
                act.wait_ge(t0, u.n + 1)
                if not u.first(2):
                    act.wait_ge(v0p, u.n - 1)
                nc.scalar.activation(h0T[p][:, :, :], bank[p][:, :], ACT.Copy).then_inc(hT0, 1)

            def exp0(u):
                p = u.p
                act.wait_ge(e0, u.n + 1)
                act.wait_ge(fd0, u.n + 1)
                if not u.first(2):
                    act.wait_ge(ud0, u.n - 1)
                for k in range(GROUP):
                    last = nc.scalar.activation(ex0[p][:, k, :], bank[2 + p][:, k * P:(k + 1) * P], ACT.Exp,
                                                bias=f0[p][:, k:k + 1])
                last.then_inc(exd0, 1)

            def apply1(u):
                p = u.p
                if not u.first(2):
                    act.wait_ge(t1, u.n - 1)
                n1.apply(nc, act, u, lambda k: X[:, u.n * PAIR + k, :], lambda k: h1n[p][:, k, :])

            skewed(act, NG, [(1, evac_hT), (2, apply0), (0, exp0)])
            apply1(FIRST_PAIR)

            def copy_hT1(u):
                p = u.p
                act.wait_ge(t1, u.n + 1)
                if not u.first(2):
                    act.wait_ge(vp1, u.n - 1)
                nc.scalar.activation(h1T[p][:, :, :], bank[4][:, 0:PAIR * P], ACT.Copy).then_inc(hT1, 1)

            def qk_hi(u):
                p = u.p
                act.wait_ge(qk1, u.n + 1)
                if not u.first(2):
                    act.wait_ge(score, CH * (u.n - 1))
                    act.wait_ge(in_k[p], H * 16 * u.i)
                nc.scalar.activation(q_hi[p][:, :, :], bank[5][:, 0:PAIR * P], ACT.Copy, scale=HD ** -0.5)
                nc.scalar.activation(k_parts[p][:, 0, :, :], bank[5][:, PAIR * P:2 * PAIR * P], ACT.Copy).then_inc(hi1, 1)

            def copy_v(u):
                p = u.p
                act.wait_ge(vp1, u.n + 1)
                if u.first(1):
                    act.wait_ge(clear1, 3)
                if not u.first(2):
                    act.wait_ge(pv, CH * (u.n - 1))
                nc.scalar.activation(v1[p][:, :, :, 0:HD],
                                     bank[4][:, PAIR * P:2 * PAIR * P].rearrange("p (g h d) -> p g h d", g=PAIR, h=H),
                                     ACT.Copy).then_inc(vd1, 1)

            def exps(j):
                def stage(u):
                    p = j % 2
                    act.wait_ge(shifted, CH * u.n + j + 1)
                    if not (u.first(1) and j < 2):
                        act.wait_ge(flip, CH * u.n + j - 1)
                    for h in range(HC):
                        last = nc.scalar.activation(prob[p][:, h, :], neg[p][:, h, :], ACT.Exp,
                                                    bias=nmax[p][:, h:h + 1], scale=-1.0)
                    last.then_inc(probD, 1)
                return stage

            def copy_last_probT(u):
                j = CH - 1
                act.wait_ge(flip, CH * u.n + j + 1)
                act.wait_ge(pv, CH * u.n + j - 1)
                nc.scalar.activation(probT[j % 2][:, :, :], bank[2 + j % 2][:, :], ACT.Copy).then_inc(flippedS, 1)

            def copy_oT1(u):
                p = u.p
                act.wait_ge(pv, CH * (u.n + 1))
                if not u.first(2):
                    act.wait_ge(back1, u.n - 1)
                nc.scalar.activation(oT1[p][:, :, :], bank[6][:, :], ACT.Copy).then_inc(oT1d, 1)

            def copy_oc1(u):
                p = u.p
                act.wait_ge(tc1, u.n + 1)
                if not u.first(2):
                    act.wait_ge(wo1, u.n - 1)
                nc.scalar.activation(oc1[p][:, :, :], bank[7][:, 0:PAIR * P], ACT.Copy).then_inc(oc1d, 1)

            skewed(act, NP, [(0, exps(1)), (-1, copy_oT1), (0, exps(2)), (2, qk_hi), (1, copy_v), (0, exps(3)), (-1, copy_oc1),
                             (3, without(1, apply1)), (1, exps(0)), (0, copy_last_probT), (3, copy_hT1)])

            act.wait_ge(soft2, 1)
            nc.scalar.activation(fexp[:, :], wt("fw"), ACT.Exp, bias=fmax[:, :], accum_out=fsum[:, :]).then_inc(soft2s, 1)

            def apply2(u):
                p = u.p
                if not u.first(2):
                    act.wait_ge(y2, 2 * (u.n - 1))
                n2.apply(nc, act, u, lambda k: tile2(u.n, k), lambda k: h2[p][:, k, :])

            act.wait_ge(x1, NP)

            def scale_columns(b):
                act.wait_ge(flip2, 2 * b + 1)
                for k in range(TILES):
                    last = nc.scalar.activation(normT[:, b, k, :], bank[2 * b][:, k * P:(k + 1) * P], ACT.Copy,
                                                scale=dinv[:, b, k:k + 1])
                last.then_inc(normD[0], 1)

            for b in range(2):
                scale_columns(b)
            apply2(FIRST_BATCH)
            for b in range(2, NB):
                scale_columns(b)

            def hidden2(u):
                for l in range(2):
                    for half in range(2):
                        act.wait_ge(hid2, 4 * u.n + 2 * l + half + 1)
                        if l == half == 0 and not u.first(1):
                            act.wait_ge(s2p, 2 * u.n)
                        for g in (range(1) if l == 0 else range(1, 5)):
                            last = nc.scalar.activation(slots(hidT[:, half, l, :], g), slots(bank[3 + 2 * l + half][:, :], g), ACT.Relu,
                                                        bias=wt("b1", 2 * g + half, 2 * g + half + 1))
                        last.then_inc(hid2d, 1)

            def outputs2(u):
                for l in range(2):
                    act.wait_ge(o2, 2 * u.n + l + 1)
                    if u.first(1):
                        act.wait_ge(soft2, 3)
                    else:
                        act.wait_ge(f2d, 3 * u.n)
                    for g in (range(1) if l == 0 else range(1, 5)):
                        last = nc.scalar.activation(slots(g2[:, l, :], g), slots(bank[5 + l][:, :], g), ACT.Relu,
                                                    bias=fwb[:, g:g + 1], scale=fw[:, g:g + 1])
                    last.then_inc(o2d, 1)

            def apply3(i, s):
                u = Unit(i, s)
                if not u.first(2):
                    act.wait_ge(aggP, nth(LAYERS * (i - 1) + 1, s))
                    act.wait_ge(flip0[s], i)
                n3.apply(nc, act, u, lambda k: X[:, u.n * GROUP + k, :], lambda k: start_n[s][:, k * P:(k + 1) * P])

            def start_hi(i, s):
                act.wait_ge(flip0[s], i + 1)
                if not (isinstance(i, int) and i == 0):
                    act.wait_ge(gateN, nth(LAYERS * i, s))
                    act.wait_ge(keptD, nth(LAYERS * (i - 1) + 1, s))
                nc.scalar.activation(h_hi[s][:, :], bank[4 * s + 3][:, :], ACT.Copy)
                nc.scalar.activation(start_T[s][:, :], bank[4 * s + 3][:, :], ACT.Copy).then_inc(startS[s], 1)

            def fold_hi(l):
                act.wait_ge(wcP, l + 1)
                nc.scalar.activation(wc_hi[:, l, :], bank[0][:, 0:GATES * P], ACT.Copy).then_inc(wcH, 1)

            def apply_layer3(u):
                if u.n == NB - 1:
                    for s in range(2):
                        apply3(0, s)

            def start_layer3(u):
                if u.n == NB - 1:
                    start_hi(0, 0)

            fold_each, fold_at_end = folds(fold_hi)
            skewed(act, NB, [fold_at_end, (0, apply_layer3), (0, outputs2), (0, start_layer3), (1, hidden2), fold_each,
                             (2, without(1, apply2))])

            def copy_state_n(i, l, s):
                act.wait_ge(flip3[s], (LAYERS - 1) * i + l)
                nc.scalar.activation(state_n[s][:, :], bank[4 * s + 3][:, :], ACT.Copy).then_inc(natural3[s], 1)

            def agg_upper(i, l, s):
                act.wait_ge(aggP, nth(LAYERS * i + l + 1, s))
                nc.scalar.activation(agg_hi[s][:, :], bank[4 * s + 2][:, :], ACT.Copy).then_inc(aggH, 1)

            def reset3(i, l, s):
                act.wait_ge(gateR, nth(LAYERS * i + l + 1, s))
                for cols in HALVES:
                    nc.scalar.activation(reset[s][:, cols], bank[4 * s][:, cols], ACT.Sigmoid, bias=brz[:, 0:1]).then_inc(resetD, 1)

            def update_gate(i, l, s):
                act.wait_ge(gateZ, nth(LAYERS * i + l + 1, s))
                nc.scalar.activation(update[s][:, :], bank[4 * s + 1][:, :], ACT.Sigmoid, bias=brz[:, 1:2]).then_inc(updateD, 1)

            def candidate(i, l, s):
                for half, cols in enumerate(HALVES):
                    act.wait_ge(preD, half_of(LAYERS * i + l + 1, s, half))
                    nc.scalar.activation(cand[s][:, cols], cand[s][:, cols], ACT.Tanh, bias=wt("bih", 2, 3)).then_inc(candD, 1)

            def turns3(i, first=False, last=False):
                for l in range(LAYERS):
                    for s in range(2):
                        post = (i, l, 0) if s else (i, l - 1, 1) if l else (i - 1, LAYERS - 1, 1)
                        busy = not (first and l == s == 0)
                        if busy:
                            reset3(*post)
                        if l:
                            copy_state_n(i, l, s)
                        if busy:
                            update_gate(*post)
                            candidate(*post)
                        agg_upper(i, l, s)
                        if l == 4 and s == 1 and not last:
                            start_hi(i + 1, 0)
                        if l == 4 and not last:
                            apply3(i + 1, s)
                        if l == 0 and s == 0:
                            start_hi(i, 1)

            turns3(0, first=True)
            with act.Fori(1, NG // 2 - 1) as i:
                turns3(i)
            turns3(NG // 2 - 1, last=True)
            post = (NG // 2 - 1, LAYERS - 1, 1)
            reset3(*post)
            update_gate(*post)
            candidate(*post)

        @block.tensor
        def _(pe):
            pe.wait_ge(w_first, 16)
            pe.wait_ge(pre0, 3)
            pe.matmul(bank[4][:, 0:P], wt("ww"), a1rep[:, :], start=True, stop=True)
            pe.matmul(bank[4][:, P:P + 1], wt("ww"), wt("acol", 1, 2), start=True, stop=True)
            pe.matmul(bank[4][:, P + 1:P + 2], brep[:, :], a12[:, :], start=True, stop=True).then_inc(prod0, 1)
            pe.wait_ge(consts, 3)

            def transpose_h(u):
                p = u.p
                pe.wait_ge(n0.done, u.n + 1)
                if not u.first(2):
                    pe.wait_ge(hT0, u.n - 1)
                for k in range(GROUP):
                    last = pe.transpose(bank[p][:, k * P:(k + 1) * P], h0n[p][:, k, :], ident[:, :])
                last.then_inc(t0, 1)

            def logits(u):
                p = u.p
                pe.wait_ge(hT0, u.n + 1)
                if u.first(1):
                    pe.wait_ge(fold0, 3)
                if not u.first(2):
                    pe.wait_ge(exd0, u.n - 1)
                pe.matmul(bank[2 + p][:, :], wa1[:, :], h0T[p][:, :, :], start=True, stop=True).then_inc(e0, 1)

            def values(u):
                p = u.p
                if not u.first(1):
                    pe.wait_ge(v0d, u.n)
                    pe.wait_ge(fd0, u.n)
                for k in range(GROUP):
                    last = pe.matmul(halves(4)[k // 2][:, k % 2, :], h0T[p][:, k, :], wplus[:, :],
                                     start=True, stop=True)
                last.then_inc(v0p, 1)

            def attend(u):
                p = u.p
                pe.wait_ge(ud0, u.n + 1)
                pe.wait_ge(v0d, u.n + 1)
                if not u.first(1):
                    pe.wait_ge(x0, u.n)
                for k in range(GROUP):
                    last = pe.matmul(halves(6)[k // 2][:, k % 2, :], u0[p][:, k, :], v0[p][:, k, :],
                                     start=True, stop=True)
                last.then_inc(o0, 1)

            skewed(pe, NG, [(0, logits), (1, transpose_h), (0, values), (-1, attend)])

            pe.wait_ge(x0, NG)
            pe.wait_ge(w_rest, 16)

            def transpose_h1(u):
                p = u.p
                pe.wait_ge(n1.done, u.n + 1)
                if not u.first(2):
                    pe.wait_ge(vd1, u.n - 1)
                for k in range(PAIR):
                    last = pe.transpose(bank[4][:, k * P:(k + 1) * P], h1n[p][:, k, :], ident[:, :])
                last.then_inc(t1, 1)

            def project_qk(u):
                p = u.p
                pe.wait_ge(hT1, u.n + 1)
                if not u.first(1):
                    pe.wait_ge(lo1, u.n)
                pe.matmul(bank[5][:, 0:PAIR * P], wt("wqT"), h1T[p][:, :, :], start=True, stop=True)
                pe.matmul(bank[5][:, PAIR * P:2 * PAIR * P], wt("wkT"), h1T[p][:, :, :], start=True, stop=True).then_inc(qk1, 1)

            def project_v(u):
                p = u.p
                for k in range(PAIR):
                    last = pe.matmul(bank[4][:, (PAIR + k) * P:(PAIR + k + 1) * P], h1T[p][:, k, :], wt("wvT"),
                                     start=True, stop=True)
                last.then_inc(vp1, 1)

            def scores(j):
                def stage(u):
                    p, g, c = u.p, j // 2, j % 2
                    to = bank[j % 2][:, :].rearrange("p (h n) -> p h n", h=HC)
                    if j == 0:
                        pe.wait_ge(hideD, u.n + 1)
                        pe.wait_ge(in_k[p], H * 16 * (u.i + 1))
                    if not (u.first(1) and j < 2):
                        pe.wait_ge(shifted, CH * u.n + j - 1)
                    heads = slice(HC * c, HC * (c + 1))
                    pe.matmul(to, ident_bf[:, :], hide[p][:, g, :].unsqueeze(1).broadcast_to([P, HC, P]), start=True, stop=False)
                    pe.matmul(to, q_hi[p][:, g, :], k_diag[p][:, 0, g, heads, :], start=False, stop=False)
                    pe.matmul(to, q_hi[p][:, g, :], k_diag[p][:, 1, g, heads, :], start=False, stop=False)
                    pe.matmul(to, q_lo[p][:, g, :], k_diag[p][:, 0, g, heads, :], start=False, stop=True).then_inc(score, 1)
                return stage

            def copied(u, j):
                if j == CH - 1:
                    pe.wait_ge(flippedS, u.n + 1)
                else:
                    pe.wait_ge(flipped, (CH - 1) * u.n + j + 1)

            def transpose_probs(j):
                def stage(u):
                    pe.wait_ge(probD, CH * u.n + j + 1)
                    if j >= 2:
                        pe.wait_ge(flipped, (CH - 1) * u.n + j - 1)
                    elif not u.first(1):
                        copied(u.back(1), j + 2)
                    for h in range(HC):
                        last = pe.transpose(bank[2 + j % 2][:, h * P:(h + 1) * P], prob[j % 2][:, h, :], ident[:, :])
                    last.then_inc(flip, 1)
                return stage

            def weigh_values(j):
                def stage(u):
                    p, g, c = u.p, j // 2, j % 2
                    copied(u, j)
                    if j == 0:
                        pe.wait_ge(vd1, u.n + 1)
                        if not u.first(1):
                            pe.wait_ge(oT1d, u.n)
                    for h in range(HC):
                        last = pe.matmul(bank[6][SLOT * h:SLOT * (h + 1), j * P:(j + 1) * P],
                                         v1[p][:, g, HC * c + h, :], probT[j % 2][:, h, :], start=True, stop=True)
                    last.then_inc(pv, 1)
                return stage

            def turn_back(u):
                p = u.p
                pe.wait_ge(oT1d, u.n + 1)
                if not u.first(1):
                    pe.wait_ge(x1, u.n)
                for j in range(CH):
                    last = pe.transpose(bank[7][:, j * P:(j + 1) * P], oT1[p][:, j, :], ident[:, :])
                last.then_inc(back1, 1)

            def transpose_o(u):
                p = u.p
                pe.wait_ge(o1d, u.n + 1)
                for k in range(PAIR):
                    last = pe.transpose(bank[7][:, k * P:(k + 1) * P],
                                        o1[p][:, k * H:(k + 1) * H, :].rearrange("p h d -> p (h d)"), ident[:, :])
                last.then_inc(tc1, 1)

            def project_o(u):
                p = u.p
                pe.wait_ge(oc1d, u.n + 1)
                for k in range(PAIR):
                    last = pe.matmul(bank[7][:, k * P:(k + 1) * P], oc1[p][:, k, :], wt("woT"), start=True, stop=True)
                last.then_inc(wo1, 1)

            skewed(pe, NP, [(0, scores(2)), (0, transpose_probs(0)), (-1, weigh_values(3)), (2, project_qk), (1, project_v),
                             (0, scores(3)), (0, transpose_probs(1)), (0, weigh_values(0)), (-1, turn_back), (1, scores(0)),
                             (0, transpose_probs(2)), (0, weigh_values(1)), (-1, transpose_o), (1, scores(1)),
                             (0, transpose_probs(3)), (0, weigh_values(2)), (-1, project_o), (3, transpose_h1)])

            def aggregate2(u):
                p = u.p
                pe.wait_ge(n2.done, u.n + 1)
                if u.first(1):
                    pe.wait_ge(normD[0], 2)
                    pe.wait_ge(normD[1], 1)
                for l in range(2):
                    if not u.first(1):
                        pe.wait_ge(s2d, 2 * u.n - 1 + l)
                    for k in range(TILES):
                        t = TILES * l + k
                        last = pe.matmul(bank[1 + l][:, k * P:(k + 1) * P], h2[p][:, t, :], normT[:, u.n, t, :], start=True, stop=True)
                    last.then_inc(y2, 1)

            def hidden_product(l):
                def stage(u):
                    pe.wait_ge(y2d, 2 * u.n + l + 1)
                    if u.first(1) and l == 0:
                        for layout in range(2):
                            pe.wait_ge(normD[layout], NB)
                    for half in range(2):
                        if not u.first(1):
                            pe.wait_ge(t2d if l == 0 else o2d, 2 * u.n - 1 + half)
                        for g in (range(1) if l == 0 else range(1, 5)):
                            at = g * HID + half * P
                            last = pe.matmul(slots(bank[3 + 2 * l + half][:, :], g), wt("w1", at, at + P), slots(yT[:, l, :], g),
                                             start=True, stop=True)
                        last.then_inc(hid2, 1)
                return stage

            def output_product(u):
                for l in range(2):
                    pe.wait_ge(hid2d, 4 * u.n + 2 * l + 2)
                    pe.wait_ge(y2d, 2 * u.n + l + 1)
                    for g in (range(1) if l == 0 else range(1, 5)):
                        for half in range(2):
                            at = (2 * g + half) * P
                            last = pe.matmul(slots(bank[1 + l][:, :], g), wt("w2", at, at + P), slots(hidT[:, half, l, :], g),
                                             start=(half == 0), stop=(half == 1))
                    last.then_inc(s2p, 1)

            def transpose_s2(u):
                for l in range(2):
                    pe.wait_ge(s2d, 2 * u.n + l + 1)
                    for k in range(TILES):
                        last = pe.transpose(bank[3 + l][:, k * P:(k + 1) * P], s2T[:, l, k * P:(k + 1) * P], ident[:, :])
                    last.then_inc(t2, 1)

            def aggregate_out(u):
                p = u.p
                for l in range(2):
                    pe.wait_ge(t2d, 2 * u.n + l + 1)
                    pe.wait_ge(hid2d, 4 * u.n + 4)
                    for k in range(TILES):
                        t = TILES * l + k
                        last = pe.matmul(bank[5 + l][:, k * P:(k + 1) * P], s2[:, t, :], normT[:, u.n, t, :], start=True, stop=True)
                    last.then_inc(o2, 1)

            def back_rows(u):
                pe.wait_ge(f2d, 3 * (u.n + 1))
                if not u.first(1):
                    pe.wait_ge(x2d, u.n)
                for k in range(TILES):
                    last = pe.transpose(bank[7][:, k * P:(k + 1) * P], f2[:, k * P:(k + 1) * P], ident[:, :])
                last.then_inc(b2, 1)

            pe.wait_ge(x1, NP)
            for i in range(2 * NB):
                b, l = i // 2, i % 2
                pe.wait_ge(rows2, b + 1)
                for k in range(TILES):
                    last = pe.transpose(bank[i][:, k * P:(k + 1) * P], a2[:, b, TILES * l + k, :], ident[:, :])
                last.then_inc(flip2, 1)
            def transpose_start(i, s):
                pe.wait_ge(n3.done, 2 * i + s + 1)
                if not (isinstance(i, int) and i == 0):
                    pe.wait_ge(dotD, half_of(LAYERS * i, s, 1))
                elif s == 1:
                    pe.wait_ge(x2d, NB)
                for k in range(GROUP):
                    last = pe.transpose(bank[4 * s + 3][:, k * P:(k + 1) * P], start_n[s][:, k * P:(k + 1) * P], ident[:, :])
                last.then_inc(flip0[s], 1)

            def fold(l):
                if l:
                    pe.wait_ge(wcD, l)
                pe.matmul(bank[0][:, 0:GATES * P], wt("gwT", l * P, (l + 1) * P), wt("wihT"), start=True, stop=True).then_inc(wcP, 1)

            def start_layer3(u):
                if u.n == NB - 1:
                    pe.wait_ge(t2d, 2 * NB)
                    transpose_start(0, 0)

            fold_each, fold_at_end = folds(fold)
            skewed(pe, NB, [fold_at_end, (0, output_product), (0, transpose_s2), (1, aggregate2), (0, aggregate_out),
                             (0, start_layer3), (1, hidden_product(0)), (0, back_rows), (1, hidden_product(1)), fold_each])

            def transpose_state(to, s, done):
                for k in range(GROUP):
                    last = pe.transpose(to[:, k * P:(k + 1) * P], state_T[s][:, k * P:(k + 1) * P], ident[:, :])
                last.then_inc(done[s], 1)

            def transpose_end(i, s, more=True):
                pe.wait_ge(stateD, nth(LAYERS * (i + 1), s))
                if more:
                    pe.wait_ge(split3[s], LAYERS * (i + 1) + 1)
                transpose_state(bank[4 * s + 3], s, flipE)

            def recurrent(s, q, passes=(0, 1, 2)):
                cols = slice(q * P, (q + 1) * P)
                for k in passes:
                    w, h = ((wh_hi, h_hi), (wh_lo, h_hi), (wh_hi, h_lo))[k]
                    pe.matmul(bank[4 * s + (q if q < 2 else 3)][:, :], w[:, cols], h[s][:, :], start=(k == 0), stop=(q == k == 2))

            def turns3(i, first=False, last=False):
                for l in range(LAYERS):
                    for s in range(2):
                        c = LAYERS * i + l
                        if l:
                            pe.wait_ge(stateD, nth(c, s))
                            transpose_state(bank[4 * s + 3], s, flip3)
                        elif not first:
                            transpose_end(i - 1, s)
                        pe.wait_ge(split3[s], c + 1)
                        recurrent(s, 0)
                        recurrent(s, 1, (0,))
                        if l == 0 and s == 0:
                            transpose_start(i, 1)
                        if l == 4 and s == 1 and not last:
                            transpose_start(i + 1, 0)
                        if l:
                            pe.wait_ge(natural3[s], (LAYERS - 1) * i + l)
                        else:
                            pe.wait_ge(edge3d[s], i + 1)
                        state = (state_n if l else start_n)[s]
                        for k in range(GROUP):
                            cols = slice(k * P, (k + 1) * P)
                            mm = pe.matmul(bank[4 * s + 2][:, cols], state[:, cols], edge3[s][:, cols], start=True, stop=True)
                        mm.then_inc(aggP, 1)
                        recurrent(s, 1, (1, 2))
                        if l == 0 and not first:
                            pe.wait_ge(x3[s], i)
                        recurrent(s, 2)
                        pe.wait_ge(aggH, nth(c + 1, s))
                        for q in range(GATES):
                            to = bank[4 * s + q][:, :]
                            cols = slice(q * P, (q + 1) * P)
                            if q == 2:
                                pe.wait_ge(aggL, nth(c + 1, s))
                            pe.matmul(to, wc_hi[:, l, cols], agg_hi[s][:, :], start=(q == 2), stop=False)
                            pe.matmul(to, wc_lo[:, l, cols], agg_hi[s][:, :], start=False, stop=False)
                        for q, ready in enumerate((gateR, gateZ, gateN)):
                            cols = slice(q * P, (q + 1) * P)
                            pe.matmul(bank[4 * s + q][:, :], wc_hi[:, l, cols], agg_lo[s][:, :], start=False,
                                      stop=True).then_inc(ready, 1)

            pe.wait_ge(whD, 2)
            pe.wait_ge(wcD, LAYERS)
            turns3(0, first=True)
            with pe.Fori(1, NG // 2 - 1) as i:
                turns3(i)
            turns3(NG // 2 - 1, last=True)
            for s in range(2):
                transpose_end(NG // 2 - 1, s, more=False)

        @block.vector
        def _(dve):
            dve.wait_ge(w_first, 16)
            nc.vector.tensor_copy(a1rep[:, :], wt("acol", 0, 1).broadcast_to([P, P])).then_inc(pre0, 1)
            nc.vector.tensor_copy(brep[:, :], wt("bcol").broadcast_to([P, P])).then_inc(pre0, 1)
            nc.vector.tensor_tensor(a12[:, :], wt("acol", 0, 1), wt("acol", 1, 2), ALU.add).then_inc(pre0, 1)
            dve.wait_ge(prod0, 1)
            nc.vector.tensor_copy(wa1[:, :], bank[4][:, 0:P]).then_inc(fold0, 1)
            nc.vector.tensor_copy(wplus[:, 0:P], wt("wwT"))
            nc.vector.tensor_copy(wplus[:, P:P + 1], bank[4][:, P:P + 1]).then_inc(fold0, 1)
            nc.vector.tensor_tensor(c0[:, :], bank[4][:, P + 1:P + 2], wt("ab"), ALU.add).then_inc(fold0, 1)

            def tile_stats0(u):
                dve.wait_ge(in_x[u.p], 16 * (u.i + 1))
                n0.tile_stats(nc, u, lambda k: X[:, u.n * GROUP + k, :], range(GROUP))

            def unit_stats0(u):
                n0.unit_stats(nc, dve, u)

            def offset0(u):
                n0.offset(nc, dve, u)

            def copy_values(u):
                p = u.p
                dve.wait_ge(v0p, u.n + 1)
                if u.first(1):
                    dve.wait_ge(fold0, 3)
                if not u.first(2):
                    dve.wait_ge(exd0, u.n - 1)
                for b in range(2):
                    last = nc.vector.tensor_scalar(f0[p][:, 2 * b:2 * b + 2], halves(4)[b][:, :, P], c0[:, :], None,
                                                   ALU.add)
                last.then_inc(fd0, 1)
                if u.first(1):
                    dve.wait_ge(consts, 3)
                if not u.first(2):
                    dve.wait_ge(o0, u.n - 1)
                for b in range(2):
                    last = nc.vector.tensor_tensor(v0[p][:, 2 * b:2 * b + 2, 0:P], halves(4)[b][:, :, 0:P],
                                                   wt("brow").unsqueeze(1).broadcast_to([P, 2, P]), ALU.add)
                last.then_inc(v0d, 1)

            def invert_sums0(u):
                p = u.p
                dve.wait_ge(o0, u.n + 1)
                for b in range(2):
                    last = nc.vector.reciprocal(r0[p][:, 2 * b:2 * b + 2], halves(6)[b][:, :, P])
                last.then_inc(rd0, 1)

            def update0(u):
                p = u.p
                dve.wait_ge(rd0, u.n + 1)
                for k in range(GROUP):
                    g = u.n * GROUP + k
                    last = nc.vector.scalar_tensor_tensor(X[:, g, :], halves(6)[k // 2][:, k % 2, 0:P], r0[p][:, k:k + 1],
                                                          X[:, g, :], ALU.mult, ALU.add)
                last.then_inc(x0, 1)

            def stats1(u):
                n1.stats(nc, dve, u, lambda k: X[:, u.n * PAIR + k, :])

            def offset1(u):
                n1.offset(nc, dve, u)

            skewed(dve, NG, [(2, offset0), (3, tile_stats0), (0, copy_values), (3, unit_stats0), (-1, invert_sums0),
                             (-1, update0), (0, when(NG - 1, stats1, FIRST_PAIR)), (-1, when(NG - 1, offset1, FIRST_PAIR)),
                             (-1, when(NG - 1, stats1, SECOND_PAIR))])

            dve.wait_ge(x0, NG)

            def hide1(u):
                p = u.p
                dve.wait_ge(in1[p], 16 * (u.i + 1))
                if not u.first(2):
                    dve.wait_ge(score, CH * (u.n - 1))
                nc.vector.tensor_scalar(hide[p][:, :, :], adj1[p][:, :, :], 0.0, MASKED, ALU.is_equal,
                                        ALU.mult).then_inc(hideD, 1)

            def qk_lo(u):
                p = u.p
                dve.wait_ge(hi1, u.n + 1)
                nc.vector.scalar_tensor_tensor(q_lo[p][:, :, :].rearrange("p g n -> p (g n)"), bank[5][:, 0:PAIR * P], HD ** -0.5,
                                               q_hi[p][:, :, :].bitcast(F32).rearrange("p g n -> p (g n)"), ALU.mult, ALU.subtract)
                nc.vector.tensor_tensor(k_parts[p][:, 1, :, :].rearrange("p g n -> p (g n)"), bank[5][:, PAIR * P:2 * PAIR * P],
                                        k_parts[p][:, 0, :, :].bitcast(F32).rearrange("p g n -> p (g n)"),
                                        ALU.subtract).then_inc(lo1, 1)

            def shift(j):
                def stage(u):
                    p, g, c = u.p, j // 2, j % 2
                    dve.wait_ge(score, CH * u.n + j + 1)
                    if j == 0:
                        dve.wait_ge(edgeD, u.n + 1)
                    if not (u.first(1) and j < 2):
                        dve.wait_ge(probD, CH * u.n + j - 1)
                    dve.sem_inc(past_dve, 1)
                    for h in range(HC):
                        last = nc.vector.tensor_tensor_reduce(
                            out=neg[j % 2][:, h, :], in0=bank[j % 2][:, h * P:(h + 1) * P],
                            in1=edge[p][:, HC * c + h, g, :], scale=-1.0, scalar=-MASKED, op0=ALU.add,
                            op1=ALU.min, accum_out=nmax[j % 2][:, h:h + 1])
                    last.then_inc(shifted, 1)
                return stage

            def copy_probT(j):
                def stage(u):
                    dve.wait_ge(flip, CH * u.n + j + 1)
                    if not (u.first(1) and j < 2):
                        dve.wait_ge(pv, CH * u.n + j - 1)
                    nc.vector.tensor_copy(probT[j % 2][:, :, :].rearrange("p h n -> p (h n)"),
                                          bank[2 + j % 2][:, :]).then_inc(flipped, 1)
                return stage

            def normalize1(u):
                p = u.p
                of = bank[7][:, :].rearrange("p (h d) -> p h d", d=SLOT)
                dve.wait_ge(back1, u.n + 1)
                nc.vector.reciprocal(r1[:, :], of[:, :, HD]).then_inc(rd1, 1)
                dve.wait_ge(rd1, u.n + 1)
                if not u.first(2):
                    dve.wait_ge(tc1, u.n - 1)
                nc.vector.tensor_tensor(o1[p][:, :, :], of[:, :, 0:HD], r1[:, :].unsqueeze(2).broadcast_to([P, PAIR * H, HD]),
                                        ALU.mult).then_inc(o1d, 1)

            def update1(u):
                dve.wait_ge(wo1, u.n + 1)
                xs = X[:, bass.ds(u.n * PAIR, PAIR), :]
                nc.vector.tensor_tensor(xs, bank[7][:, 0:PAIR * P].rearrange("p (g n) -> p g n", g=PAIR), xs,
                                        ALU.add).then_inc(x1, 1)

            def degrees(u):
                if isinstance(u.i, int) and u.n < NB:
                    b = u.n
                    if b == 0:
                        dve.wait_ge(in_a2, 16)
                    nc.vector.tensor_tensor(a2[:, b, :, :], a2[:, b, :, :], ident[:, :].unsqueeze(1).broadcast_to([P, T2, P]),
                                            ALU.add).then_inc(plus2, 1)
                    dve.wait_ge(plus2, 2 * b + 1)
                    nc.vector.tensor_reduce(deg[:, b, :], a2[:, b, :, :], AXIS.X, ALU.add).then_inc(plus2, 1)
                    dve.wait_ge(plus2, 2 * b + 2)
                    nc.vector.scalar_tensor_tensor(degs[:, b, :], deg[:, b, :], 0.0, deg[:, b, :], ALU.is_equal,
                                                   ALU.add).then_inc(degD, 1)

            def scale_rows(u):
                if isinstance(u.i, int) and u.n < NB:
                    b = u.n
                    dve.wait_ge(degp, b + 1)
                    nc.vector.scalar_tensor_tensor(dinv[:, b, :], deg[:, b, :], 0.0, dpow[:, b, :], ALU.not_equal,
                                                   ALU.mult).then_inc(dinvD, 1)
                    dve.wait_ge(dinvD, b + 1)
                    for t in range(T2):
                        last = nc.vector.tensor_scalar(a2[:, b, t, :], a2[:, b, t, :], dinv[:, b, t:t + 1], None, ALU.mult)
                    last.then_inc(rows2, 1)

            def stats2(u):
                p = u.p
                dve.wait_ge(in_x2, GATHERS * (u.n + 1))
                n2.stats(nc, dve, u, lambda k: tile2(u.n, k))

            def offset2(u):
                n2.offset(nc, dve, u)

            skewed(dve, NP, [(-2, update1), (0, copy_probT(0)), (1, hide1), (0, shift(2)), (0, shift(3)), (0, copy_probT(1)),
                             (-1, normalize1), (3, without(1, offset1)), (2, qk_lo), (0, copy_probT(2)), (1, shift(0)),
                             (4, without(2, stats1)), (1, shift(1)), (4, degrees), (2, scale_rows),
                             (0, when(NP - 1, stats2, FIRST_BATCH)), (-1, when(NP - 1, offset2, FIRST_BATCH))])

            dve.wait_ge(x1, NP)
            nc.vector.tensor_reduce(fmax[:, :], wt("fw"), AXIS.X, ALU.max, negate=True).then_inc(soft2, 1)
            dve.wait_ge(soft2s, 1)
            nc.vector.reciprocal(frec[:, :], fsum[:, :]).then_inc(soft2, 1)
            dve.wait_ge(soft2, 2)
            nc.vector.tensor_scalar(fw[:, :], fexp[:, :], frec[:, :], None, ALU.mult)
            nc.vector.scalar_tensor_tensor(fwb[:, :], fexp[:, :], frec[:, :], wt("b2"), ALU.mult, ALU.mult).then_inc(soft2, 1)

            def copy_y(u):
                for l in range(2):
                    dve.wait_ge(y2, 2 * u.n + l + 1)
                    if not u.first(1):
                        dve.wait_ge(hid2, 4 * u.n)
                    nc.vector.tensor_copy(yT[:, l, :], bank[1 + l][:, :]).then_inc(y2d, 1)

            def copy_s2T(u):
                for l in range(2):
                    dve.wait_ge(s2p, 2 * u.n + l + 1)
                    if not u.first(1):
                        dve.wait_ge(t2, 2 * u.n)
                    for lo, hi in ([(0, NN)] if l == 0 else [(0, 16), (18, 30)]):
                        last = nc.vector.tensor_copy(rows_of(s2T[:, l, :])[:, :, lo:hi], rows_of(bank[1 + l][:, :])[:, :, lo:hi])
                    last.then_inc(s2d, 1)

            def copy_s2(u):
                for l in range(2):
                    dve.wait_ge(t2, 2 * u.n + l + 1)
                    if not u.first(1):
                        dve.wait_ge(o2, 2 * u.n)
                    nc.vector.tensor_copy(s2[:, TILES * l:TILES * (l + 1), :].rearrange("p t c -> p (t c)"),
                                          bank[3 + l][:, :]).then_inc(t2d, 1)

            def fuse(u):
                a, b = rows_of(g2[:, 0, :]), rows_of(g2[:, 1, :])
                f, fa = rows_of(f2[:, :]), rows_of(f2a[:, :])
                dve.wait_ge(o2d, 2 * u.n + 2)
                if u.first(1):
                    dve.wait_ge(clear3, 1)
                else:
                    dve.wait_ge(b2, u.n)
                nc.vector.tensor_tensor(fa[:, :, 0:15], a[:, :, 0:15], b[:, :, 0:15], ALU.add)
                nc.vector.tensor_copy(f[:, :, 15:NN], a[:, :, 15:NN]).then_inc(f2d, 1)
                dve.wait_ge(f2d, 3 * u.n + 1)
                nc.vector.tensor_tensor(f[:, :, 0:1], fa[:, :, 0:1], b[:, :, 15:16], ALU.add)
                nc.vector.tensor_copy(f[:, :, 1:3], fa[:, :, 1:3]).then_inc(f2d, 1)
                nc.vector.tensor_tensor(f[:, :, 3:15], fa[:, :, 3:15], b[:, :, 18:30], ALU.add).then_inc(f2d, 1)

            def update2(u):
                p = u.p
                dve.wait_ge(b2, u.n + 1)
                if not u.first(2):
                    dve.wait_ge(out2[p], 64 * u.i)
                nc.vector.tensor_tensor(xn2[p][:, :, :].rearrange("p t c -> p (t c)"), bank[7][:, :],
                                        x2[:, 0, TILES * u.n:TILES * (u.n + 1), :].rearrange("p t c -> p (t c)"), ALU.add).then_inc(x2d, 1)

            def stats3(i, s):
                u = Unit(i, s)
                n3.stats(nc, dve, u, lambda k: X[:, u.n * GROUP + k, :])

            def next_stats(i, l, s):
                u = Unit(i, s)
                if l in (1, 2):
                    n3.tile_stats(nc, u, lambda k: X[:, u.n * GROUP + k, :], range(2 * l - 2, 2 * l))
                elif l == 3:
                    n3.unit_stats(nc, dve, u)
                elif l == 4:
                    offset3(i, s)

            def offset3(i, s):
                n3.offset(nc, dve, Unit(i, s))

            def edges3(i, s):
                dve.wait_ge(in3[s], 16 * (i + 1))
                if not (isinstance(i, int) and i == 0):
                    dve.wait_ge(aggP, nth(LAYERS * i, s))
                nc.vector.tensor_scalar(edge3[s][:, :], adj3[s][:, :], 0.0, None, ALU.not_equal).then_inc(edge3d[s], 1)

            def start_rest(i, s):
                dve.wait_ge(startS[s], i + 1)
                nc.vector.tensor_tensor(h_lo[s][:, :], bank[4 * s + 3][:, :], h_hi[s][:, :].bitcast(F32),
                                        ALU.subtract).then_inc(split3[s], 1)

            for b in range(NB):
                dve.wait_ge(flip2, 2 * b + 2)
                for k in range(TILES):
                    t = TILES + k
                    last = nc.vector.tensor_scalar(normT[:, b, t, :], bank[2 * b + 1][:, k * P:(k + 1) * P],
                                                   dinv[:, b, t:t + 1], None, ALU.mult)
                last.then_inc(normD[1], 1)

            nc.vector.tensor_copy(wh_hi[:, :], wt("whhT")).then_inc(whD, 1)
            nc.vector.tensor_tensor(brz[:, :], wt("bih"), wt("bhh"), ALU.add)
            dve.wait_ge(whD, 1)
            nc.vector.tensor_tensor(wh_lo[:, :], wt("whhT"), wh_hi[:, :].bitcast(F32), ALU.subtract).then_inc(whD, 1)

            def fold_lo(l):
                dve.wait_ge(wcH, l + 1)
                nc.vector.tensor_tensor(wc_lo[:, l, :], bank[0][:, 0:GATES * P], wc_hi[:, l, :].bitcast(F32),
                                        ALU.subtract).then_inc(wcD, 1)

            def start_layer3(u):
                if u.n == NB - 2:
                    dve.wait_ge(out2[0], 64)
                    for s in range(2):
                        stats3(0, s)
                    for s in range(2):
                        offset3(0, s)

            fold_each, fold_at_end = folds(fold_lo)
            skewed(dve, NB, [(0, copy_s2T), (0, copy_s2), (1, copy_y), fold_at_end, (2, without(1, offset2)), (0, fuse),
                             (0, update2), (3, without(1, stats2)), fold_each, (0, start_layer3)])
            start_rest(0, 0)
            for s in range(2):
                edges3(0, s)

            def agg_lower(i, l, s):
                dve.wait_ge(aggH, nth(LAYERS * i + l + 1, s))
                nc.vector.tensor_tensor(agg_lo[s][:, :], bank[4 * s + 2][:, :], agg_hi[s][:, :].bitcast(F32),
                                        ALU.subtract).then_inc(aggL, 1)

            def pre_candidate(i, l, s):
                c = LAYERS * i + l
                dve.wait_ge(gateN, nth(c + 1, s))
                for half, cols in enumerate(HALVES):
                    dve.wait_ge(resetD, half_of(c + 1, s, half))
                    nc.vector.scalar_tensor_tensor(mixed[s][:, cols], bank[4 * s + 3][:, cols], wt("bhh", 2, 3), reset[s][:, cols],
                                                   ALU.add, ALU.mult).then_inc(dotD, 1)
                for half, cols in enumerate(HALVES):
                    dve.wait_ge(dotD, half_of(c + 1, s, half))
                    nc.vector.tensor_tensor(cand[s][:, cols], bank[4 * s + 2][:, cols], mixed[s][:, cols], ALU.add).then_inc(preD, 1)

            def mix(i, l, s):
                c = LAYERS * i + l
                dve.wait_ge(updateD, nth(c + 1, s))
                for half, cols in enumerate(HALVES):
                    dve.wait_ge(candD, half_of(c + 1, s, half))
                    nc.vector.scalar_tensor_tensor(mixed[s][:, cols], update[s][:, cols], -1.0, cand[s][:, cols],
                                                   ALU.add, ALU.mult).then_inc(mixD, 1)

            def new_state(i, l, s):
                c = LAYERS * i + l
                dve.wait_ge(keptD, nth(c + 1, s))
                for half, cols in enumerate(HALVES):
                    dve.wait_ge(mixD, half_of(c + 1, s, half))
                    last_state = nc.vector.tensor_tensor(state_T[s][:, cols], kept[s][:, cols], mixed[s][:, cols], ALU.subtract)
                last_state.then_inc(stateD, 1)

            def split_state(i, l, s):
                c = LAYERS * i + l
                if l < LAYERS - 1:
                    dve.wait_ge(stateD, nth(c + 1, s))
                    nc.vector.tensor_copy(h_hi[s][:, :], state_T[s][:, :]).then_inc(hiD, 1)
                    dve.wait_ge(hiD, nth((LAYERS - 1) * i + l + 1, s))
                    nc.vector.tensor_tensor(h_lo[s][:, :], state_T[s][:, :], h_hi[s][:, :].bitcast(F32),
                                            ALU.subtract).then_inc(split3[s], 1)

            def update3(i, s):
                dve.wait_ge(flipE[s], i + 1)
                for k in range(GROUP):
                    g = (2 * i + s) * GROUP + k
                    at = (2 * i + s) * GROUP + k
                    last = nc.vector.scalar_tensor_tensor(X[:, g, :], bank[4 * s + 3][:, k * P:(k + 1) * P],
                                                          weights[:, bass.ds(COL["nmask"][0] + at, 1)], X[:, g, :], ALU.mult, ALU.add)
                last.then_inc(x3[s], 1)

            def turns3(i, first=False, last=False):
                for l in range(LAYERS):
                    for s in range(2):
                        post = (i, l, 0) if s else (i, l - 1, 1) if l else (i - 1, LAYERS - 1, 1)
                        busy = not (first and l == s == 0)
                        if busy:
                            pre_candidate(*post)
                        if l == 0 and not first:
                            update3(i - 1, s)
                        if not last:
                            next_stats(i + 1, l, s)
                        if busy:
                            mix(*post)
                        agg_lower(i, l, s)
                        if busy:
                            new_state(*post)
                        if busy:
                            split_state(*post)
                        if l == 0 and s == 0:
                            start_rest(i, 1)
                            if not first:
                                edges3(i, 1)
                        if l == 4 and s == 1 and not last:
                            start_rest(i + 1, 0)
                            edges3(i + 1, 0)

            turns3(0, first=True)
            for p in range(2):
                dve.wait_ge(out2[p], 64 * NB // 2)
            with dve.Fori(1, NG // 2 - 1) as i:
                turns3(i)
            turns3(NG // 2 - 1, last=True)
            post = (NG // 2 - 1, LAYERS - 1, 1)
            pre_candidate(*post)
            mix(*post)
            new_state(*post)
            for s in range(2):
                update3(NG // 2 - 1, s)


def kernel(**inputs):
    import concourse.bacc as _bacc
    from concourse.bass_utils import run_bass_kernel_spmd as _run

    a = {k: np.asarray(v) for k, v in inputs.items()}
    x, adj = a["x"], a["adj"]

    def rows(v):
        return np.broadcast_to(v.reshape(1, -1), (P, v.size))

    W1, W2 = a["L2_gnn_W1"], a["L2_gnn_W2"]
    part = {
        "ww": a["L0_gnn_W_w"], "wwT": a["L0_gnn_W_w"].T, "bcol": a["L0_gnn_W_b"][:, None],
        "acol": a["L0_gnn_a_w"].reshape(2, P).T, "ab": rows(a["L0_gnn_a_b"]), "brow": rows(a["L0_gnn_W_b"]),
        "wqT": a["L1_gnn_W_q"].T, "wkT": a["L1_gnn_W_k"].T, "wvT": a["L1_gnn_W_v"].T, "woT": a["L1_gnn_W_o"].T,
        "we": rows(a["L1_gnn_W_e"]),
        "w1": W1.transpose(1, 0, 2).reshape(P, -1), "b1": a["L2_gnn_b1"].reshape(10, P).T,
        "w2": W2.reshape(10, P, P).transpose(1, 0, 2).reshape(P, -1), "b2": a["L2_gnn_b2"].T,
        "fw": rows(a["L2_gnn_fusion_w"]),
        "gwT": a["L3_gnn_weight"].transpose(2, 0, 1).reshape(P, -1),
        "wihT": a["L3_gnn_w_ih"].T, "whhT": a["L3_gnn_w_hh"].T,
        "bih": a["L3_gnn_b_ih"].reshape(GATES, P).T, "bhh": a["L3_gnn_b_hh"].reshape(GATES, P).T,
        "nmask": a["nodemask"].T,
    }
    arrays = {
        "x": x.transpose(1, 0, 2), "adj": adj.transpose(1, 0, 2), "adjT": adj.transpose(2, 0, 1),
        "weights": np.concatenate([part[n] for n, _ in _SIZES], axis=1), "blocks": pack_blocks(adj).reshape(P, -1),
    }
    arrays = {k: np.ascontiguousarray(v) for k, v in arrays.items()}
    nc = _bacc.Bacc("TRN2", target_bir_lowering=False, num_devices=1)
    ins = {k: nc.dram_tensor(f"in_{k}", v.shape, mybir.dt.from_np(v.dtype), kind="ExternalInput").ap()
           for k, v in arrays.items()}
    out = nc.dram_tensor("out", (P, B, P), F32, kind="ExternalOutput").ap()
    build(nc, ins, out)
    r = _run(nc, [{f"in_{k}": v for k, v in arrays.items()}], core_ids=[0])
    return np.ascontiguousarray(r.results[0]["out"].transpose(1, 0, 2))


def pack_blocks(adj):
    packed = np.zeros((P, NB, 2, TILES, P), adj.dtype)
    for b in range(B):
        batch, tile, s = b // BG, b % BG // 4, b % 4 * SLOT
        packed[s:s + NN, batch, 0, tile, s:s + NN] = adj[b, :NN, :NN]
        for r, n, g in ROWS:
            for c, m, k in ROWS:
                if g == k:
                    packed[s + r, batch, 1, tile, s + c] = adj[b, n, m]
    return packed
```
